# Optimizing a Trainium2 kernel written in Bass

```python
import numpy as np
import jax
import jax.numpy as jnp

def _softmax(x, axis=-1):
    return jax.nn.softmax(x, axis=axis)

def _gelu(x):
    return jax.nn.gelu(x, approximate=True)

def _silu(x):
    return jax.nn.silu(x)

def _sigmoid(x):
    return jax.nn.sigmoid(x)

def _layernorm(x, axis=-1, eps=1e-05):
    m = jnp.mean(x, axis=axis, keepdims=True)
    v = jnp.var(x, axis=axis, keepdims=True)
    return (x - m) / jnp.sqrt(v + eps)

def _scatter_add(tgt, idx, src, axis=0):
    return tgt.at[idx].add(src)

def _segment_sum(src, seg, n):
    return jax.ops.segment_sum(src, seg, n)
kernel_name = 'mk_seq_preln_d1_jaxref_r8_a9734f'

def setup_inputs(seed: int=0):
    np.random.seed(seed)
    _w = jnp.asarray

    def _L0_attn_setup():
        import jax, jax.numpy as jnp
        import numpy as np
        D_MODEL = 128
        N_HEAD = 16
        HEAD_DIM = D_MODEL // N_HEAD
        D_INNER = 512
        N_LAYER = 4
        NEG = jnp.finfo(jnp.float32).min

        def _ln(x, w, b):
            m = x.mean(-1, keepdims=True)
            v = ((x - m) ** 2).mean(-1, keepdims=True)
            return (x - m) * jax.lax.rsqrt(v + 1e-06) * w + b

        def _pos_emb(k_len):
            pos = jnp.arange(k_len - 1, -1, -1, dtype=jnp.float32)
            inv = 1.0 / 10000.0 ** (jnp.arange(0, HEAD_DIM, 2, dtype=jnp.float32) / HEAD_DIM)
            s = pos[:, None] * inv[None, :]
            return jnp.concatenate([jnp.sin(s), jnp.cos(s)], axis=-1)

        def _rel_shift(x, q_len, k_len):
            B, H = (x.shape[0], x.shape[1])
            zp = jnp.zeros((B, H, q_len, 1), x.dtype)
            xp = jnp.concatenate([zp, x], axis=-1).reshape(B, H, k_len + 1, q_len)
            return xp[:, :, 1:, :].reshape(B, H, q_len, k_len)

        def _attn(xn, Wq, bq, Wk, bk, Wv, bv, Wo, bo, u):
            B, S, _ = xn.shape
            sh = lambda t: t.reshape(B, S, N_HEAD, HEAD_DIM).transpose(0, 2, 1, 3)
            q = sh(xn @ Wq.T + bq)
            k = sh(xn @ Wk.T + bk)
            v = sh(xn @ Wv.T + bv)
            scores = jnp.einsum('bhqd,bhkd->bhqk', q, k)
            r = _pos_emb(S)
            rel = jnp.einsum('bhqd,ld->bhql', q + u[None, :, None, :], r)
            scores = (scores + _rel_shift(rel, S, S)) * HEAD_DIM ** (-0.5)
            mask = jnp.arange(S)[None, :] > jnp.arange(S)[:, None]
            scores = jnp.where(mask[None, None], NEG, scores)
            p = jax.nn.softmax(scores, axis=-1)
            ctx = jnp.einsum('bhqk,bhkd->bhqd', p, v).transpose(0, 2, 1, 3).reshape(B, S, D_MODEL)
            return ctx @ Wo.T + bo
        key = jax.random.key(seed)
        ks = jax.random.split(key, 20)
        B, S = (4, 128)
        p = lambda k, shp, s=0.02: jax.random.normal(k, shp, dtype=jnp.float32) * s
        L = N_LAYER
        return {'x': jax.random.normal(ks[0], (B, S, D_MODEL), dtype=jnp.float32), 'Wq': p(ks[1], (L, D_MODEL, D_MODEL)), 'bq': jnp.zeros((L, D_MODEL)), 'Wk': p(ks[2], (L, D_MODEL, D_MODEL)), 'bk': jnp.zeros((L, D_MODEL)), 'Wv': p(ks[3], (L, D_MODEL, D_MODEL)), 'bv': jnp.zeros((L, D_MODEL)), 'Wo': p(ks[4], (L, D_MODEL, D_MODEL)), 'bo': jnp.zeros((L, D_MODEL)), 'u_bias': p(ks[5], (L, N_HEAD, HEAD_DIM), 0.02), 'W1': p(ks[6], (L, D_INNER, D_MODEL)), 'b1': jnp.zeros((L, D_INNER)), 'W2': p(ks[7], (L, D_MODEL, D_INNER)), 'b2': jnp.zeros((L, D_MODEL)), 'ln1_w': jnp.ones((L, D_MODEL)), 'ln1_b': jnp.zeros((L, D_MODEL)), 'ln2_w': jnp.ones((L, D_MODEL)), 'ln2_b': jnp.zeros((L, D_MODEL))}
    _L0_attn_in = _L0_attn_setup()

    def _L0_ffn_setup():
        import jax, jax.numpy as jnp
        import numpy as np
        import math
        D_MODEL, D_FF, N_EXPERTS, TOP_K, N_SHARED = (128, 512, 8, 2, 1)
        B, T = (4, 128)
        SCALE = 1.0 / math.sqrt(N_SHARED + TOP_K / N_EXPERTS)
        key = jax.random.key(seed)
        ks = jax.random.split(key, 10)
        s1 = 1.0 / math.sqrt(D_MODEL)
        s2 = 1.0 / math.sqrt(D_FF)
        return {'x': jax.random.normal(ks[0], (B, T, D_MODEL), dtype=jnp.float32), 'w_router': jax.random.normal(ks[1], (N_EXPERTS, D_MODEL), dtype=jnp.float32) * s1, 'W1': jax.random.normal(ks[2], (N_EXPERTS, D_FF, D_MODEL), dtype=jnp.float32) * s1, 'b1': jax.random.normal(ks[3], (N_EXPERTS, D_FF), dtype=jnp.float32) * 0.02, 'W2': jax.random.normal(ks[4], (N_EXPERTS, D_MODEL, D_FF), dtype=jnp.float32) * s2, 'b2': jax.random.normal(ks[5], (N_EXPERTS, D_MODEL), dtype=jnp.float32) * 0.02, 'Ws1': jax.random.normal(ks[6], (D_FF, D_MODEL), dtype=jnp.float32) * s1, 'bs1': jax.random.normal(ks[7], (D_FF,), dtype=jnp.float32) * 0.02, 'Ws2': jax.random.normal(ks[8], (D_MODEL, D_FF), dtype=jnp.float32) * s2, 'bs2': jax.random.normal(ks[9], (D_MODEL,), dtype=jnp.float32) * 0.02}
    _L0_ffn_in = _L0_ffn_setup()
    _d = {'L0_attn_x': _L0_attn_in['x'], 'L0_attn_Wq': _L0_attn_in['Wq'], 'L0_attn_bq': _L0_attn_in['bq'], 'L0_attn_Wk': _L0_attn_in['Wk'], 'L0_attn_bk': _L0_attn_in['bk'], 'L0_attn_Wv': _L0_attn_in['Wv'], 'L0_attn_bv': _L0_attn_in['bv'], 'L0_attn_Wo': _L0_attn_in['Wo'], 'L0_attn_bo': _L0_attn_in['bo'], 'L0_attn_u_bias': _L0_attn_in['u_bias'], 'L0_attn_W1': _L0_attn_in['W1'], 'L0_attn_b1': _L0_attn_in['b1'], 'L0_attn_W2': _L0_attn_in['W2'], 'L0_attn_b2': _L0_attn_in['b2'], 'L0_attn_ln1_w': _L0_attn_in['ln1_w'], 'L0_attn_ln1_b': _L0_attn_in['ln1_b'], 'L0_attn_ln2_w': _L0_attn_in['ln2_w'], 'L0_attn_ln2_b': _L0_attn_in['ln2_b'], 'L0_ffn_w_router': _L0_ffn_in['w_router'], 'L0_ffn_W1': _L0_ffn_in['W1'], 'L0_ffn_b1': _L0_ffn_in['b1'], 'L0_ffn_W2': _L0_ffn_in['W2'], 'L0_ffn_b2': _L0_ffn_in['b2'], 'L0_ffn_Ws1': _L0_ffn_in['Ws1'], 'L0_ffn_bs1': _L0_ffn_in['bs1'], 'L0_ffn_Ws2': _L0_ffn_in['Ws2'], 'L0_ffn_bs2': _L0_ffn_in['bs2']}
    _x0 = _d['L0_attn_x']
    _d['L0_attn_x'] = jax.random.normal(jax.random.fold_in(jax.random.key(seed), 1), (2, 1024, 128), dtype=_x0.dtype)
    del _x0
    return _d

def reference(L0_attn_x, L0_attn_Wq, L0_attn_bq, L0_attn_Wk, L0_attn_bk, L0_attn_Wv, L0_attn_bv, L0_attn_Wo, L0_attn_bo, L0_attn_u_bias, L0_attn_W1, L0_attn_b1, L0_attn_W2, L0_attn_b2, L0_attn_ln1_w, L0_attn_ln1_b, L0_attn_ln2_w, L0_attn_ln2_b, L0_ffn_w_router, L0_ffn_W1, L0_ffn_b1, L0_ffn_W2, L0_ffn_b2, L0_ffn_Ws1, L0_ffn_bs1, L0_ffn_Ws2, L0_ffn_bs2):

    def _L0_attn_ref(x, Wq, bq, Wk, bk, Wv, bv, Wo, bo, u_bias, W1, b1, W2, b2, ln1_w, ln1_b, ln2_w, ln2_b):
        import jax, jax.numpy as jnp
        import numpy as np
        D_MODEL = 128
        N_HEAD = 16
        HEAD_DIM = D_MODEL // N_HEAD
        D_INNER = 512
        N_LAYER = 4
        NEG = jnp.finfo(jnp.float32).min

        def _ln(x, w, b):
            m = x.mean(-1, keepdims=True)
            v = ((x - m) ** 2).mean(-1, keepdims=True)
            return (x - m) * jax.lax.rsqrt(v + 1e-06) * w + b

        def _pos_emb(k_len):
            pos = jnp.arange(k_len - 1, -1, -1, dtype=jnp.float32)
            inv = 1.0 / 10000.0 ** (jnp.arange(0, HEAD_DIM, 2, dtype=jnp.float32) / HEAD_DIM)
            s = pos[:, None] * inv[None, :]
            return jnp.concatenate([jnp.sin(s), jnp.cos(s)], axis=-1)

        def _rel_shift(x, q_len, k_len):
            B, H = (x.shape[0], x.shape[1])
            zp = jnp.zeros((B, H, q_len, 1), x.dtype)
            xp = jnp.concatenate([zp, x], axis=-1).reshape(B, H, k_len + 1, q_len)
            return xp[:, :, 1:, :].reshape(B, H, q_len, k_len)

        def _attn(xn, Wq, bq, Wk, bk, Wv, bv, Wo, bo, u):
            B, S, _ = xn.shape
            sh = lambda t: t.reshape(B, S, N_HEAD, HEAD_DIM).transpose(0, 2, 1, 3)
            q = sh(xn @ Wq.T + bq)
            k = sh(xn @ Wk.T + bk)
            v = sh(xn @ Wv.T + bv)
            scores = jnp.einsum('bhqd,bhkd->bhqk', q, k)
            r = _pos_emb(S)
            rel = jnp.einsum('bhqd,ld->bhql', q + u[None, :, None, :], r)
            scores = (scores + _rel_shift(rel, S, S)) * HEAD_DIM ** (-0.5)
            mask = jnp.arange(S)[None, :] > jnp.arange(S)[:, None]
            scores = jnp.where(mask[None, None], NEG, scores)
            p = jax.nn.softmax(scores, axis=-1)
            ctx = jnp.einsum('bhqk,bhkd->bhqd', p, v).transpose(0, 2, 1, 3).reshape(B, S, D_MODEL)
            return ctx @ Wo.T + bo
        h = x
        for l in range(N_LAYER):
            xn = _ln(h, ln1_w[l], ln1_b[l])
            a = _attn(xn, Wq[l], bq[l], Wk[l], bk[l], Wv[l], bv[l], Wo[l], bo[l], u_bias[l])
            h = h + a
            fn = _ln(h, ln2_w[l], ln2_b[l])
            ff = jax.nn.gelu(fn @ W1[l].T + b1[l], approximate=False) @ W2[l].T + b2[l]
            h = h + ff
        return h

    def _L0_ffn_ref(x, w_router, W1, b1, W2, b2, Ws1, bs1, Ws2, bs2):
        import jax, jax.numpy as jnp
        import numpy as np
        import math
        D_MODEL, D_FF, N_EXPERTS, TOP_K, N_SHARED = (128, 512, 8, 2, 1)
        B, T = (4, 128)
        SCALE = 1.0 / math.sqrt(N_SHARED + TOP_K / N_EXPERTS)
        logits = jnp.einsum('btd,ed->bte', x, w_router)
        probs = jax.nn.softmax(logits, axis=-1)
        vals, idx = jax.lax.top_k(probs, TOP_K)
        gates = jnp.sum(jax.nn.one_hot(idx, N_EXPERTS, dtype=x.dtype) * vals[..., None], axis=-2)
        hs = jax.nn.gelu(jnp.einsum('btd,fd->btf', x, Ws1) + bs1)
        acc = jnp.einsum('btf,df->btd', hs, Ws2) + bs2
        h = jax.nn.gelu(jnp.einsum('btd,efd->btef', x, W1) + b1)
        y = jnp.einsum('btef,edf->bted', h, W2) + b2
        acc = acc + jnp.einsum('bted,bte->btd', y, gates)
        return SCALE * acc
    x = L0_attn_x
    x = x + _L0_attn_ref(_layernorm(x, axis=-1), L0_attn_Wq, L0_attn_bq, L0_attn_Wk, L0_attn_bk, L0_attn_Wv, L0_attn_bv, L0_attn_Wo, L0_attn_bo, L0_attn_u_bias, L0_attn_W1, L0_attn_b1, L0_attn_W2, L0_attn_b2, L0_attn_ln1_w, L0_attn_ln1_b, L0_attn_ln2_w, L0_attn_ln2_b)
    x = x + _L0_ffn_ref(_layernorm(x, axis=-1), L0_ffn_w_router, L0_ffn_W1, L0_ffn_b1, L0_ffn_W2, L0_ffn_b2, L0_ffn_Ws1, L0_ffn_bs1, L0_ffn_Ws2, L0_ffn_bs2)
    return x

_drawn_inputs = setup_inputs


def setup_inputs(seed=0):
    import zlib

    import numpy as np

    out = dict(_drawn_inputs(seed))
    spreads = {'L0_attn_bq': (0.0, 0.8),
     'L0_attn_bk': (0.0, 2.0),
     'L0_attn_bv': (0.0, 0.331),
     'L0_attn_bo': (0.0, 0.1),
     'L0_attn_b1': (0.0, 0.303),
     'L0_attn_b2': (0.0, 0.1),
     'L0_attn_ln1_w': (1.0, 0.6),
     'L0_attn_ln1_b': (0.0, 0.8),
     'L0_attn_ln2_w': (1.0, 0.6),
     'L0_attn_ln2_b': (0.0, 0.8)}
    factors = {'L0_attn_Wq': 8.0,
     'L0_attn_Wk': 8.0,
     'L0_attn_Wv': 4.356,
     'L0_attn_u_bias': 34.1,
     'L0_ffn_b1': 22.301,
     'L0_ffn_b2': 8.0,
     'L0_ffn_bs1': 8.0,
     'L0_ffn_bs2': 5.965}
    for name, (base, spread) in spreads.items():
        noise = np.random.default_rng([zlib.crc32(name.encode()), seed]).standard_normal(out[name].shape)
        drawn = base * np.exp(spread * noise) if base else spread * noise
        out[name] = jnp.asarray(drawn.astype(out[name].dtype))
    for name, factor in factors.items():
        out[name] = (out[name] * factor).astype(out[name].dtype)
    return out
```

```python
import concourse.bass as bass
from concourse import mybir
from contextlib import ExitStack
import numpy as np

F32 = mybir.dt.float32
BF16 = mybir.dt.bfloat16
I32 = mybir.dt.int32
ALU = mybir.AluOpType
ACT = mybir.ActivationFunctionType
AX = mybir.AxisListType

B, S, D = 2, 1024, 128
L, NH, DH = 4, 16, 8
FF, E = 512, 8
P = 128
QT = S // P
BLK = 512
NB = S // BLK
TB = BLK // P
G = 4
NQ = NH // G
FT = FF // P
NT = B * QT
EXPERTS = E + 1
SCALE = float(DH) ** -0.5
MOE_SCALE = 1.0 / float(np.sqrt(1 + 2 / E))
NEG = -3.0e38
EPS_OUT, EPS_LAYER = 1e-5, 1e-6

Q_PARTS = (0, 0, 0, 1, 1, 2)
K_PARTS = (0, 1, 2, 0, 1, 0)
NP = len(Q_PARTS)
REL = NP * DH
SHIFT = 2 * REL
ROWS = SHIFT + 2

UNITS = [(b, t) for b in range(NB) for t in range(TB * (b + 1))]
CHUNKS = [(3, 0, 512), (4, 0, 512), (5, 0, 512), (2, 0, 384), (6, 0, 512), (7, 0, 512), (7, 512, 512),
          (6, 512, 384), (1, 0, 256), (5, 512, 256), (0, 0, 128), (4, 512, 128)]
NU = len(UNITS)
AHEAD = NU + 3
LAG = 2
RING = 4

V_COLS = DH + 1
A_USES, A_ACT, A_DVE, A_POOL, A_SPLIT = 10, 8, 2, 14, 12
D_USES, D_ACT, D_DVE = 14, 12, 4
NEWTON = 3
LN_OPS = 2 * QT + 3 + 4 * NEWTON
VA, VD = 8, 8


def diagonal(u):
    b, t = UNITS[u]
    return t >= TB * b


def span(u):
    b, t = UNITS[u]
    first = max(0, t - TB * b) * P
    return first, BLK - first


MASKED = [u for u in range(NU) if diagonal(u)]


def build(nc, x_d, wa_d, va_d, wd_d, vd_d, rows_d, wr_d, we_d, be_d, ident_d, identb_d, maskb_d, rot_d, kst_d,
          out_d):
    ctx = ExitStack()
    with ctx:
        def sb(name, shape, dt=F32):
            return ctx.enter_context(nc.sbuf_tensor(name, shape, dt))

        def sem(name):
            return ctx.enter_context(nc.semaphore(name))

        scratch = nc.dram_tensor("split_scratch", [B, 3, 3, D, S], BF16, kind="Internal").ap()

        q_stack = sb("q_stack", [P, NQ, G, S], BF16)
        k_stack = sb("k_stack", [P, NQ, G, S], BF16)
        probs = sb("probs", [P, RING, G, BLK])
        values = sb("values", [P, B, QT, NH, V_COLS])
        h = sb("h", [P, NT, D])
        xn_t = sb("xn_t", [P, S])
        d_t = sb("d_t", [P, S])
        centred = sb("centred", [P, QT, D])
        rot = sb("rot", [P, 2, S])
        split = sb("split", [P, NB, 3, 3, BLK], BF16)
        work = sb("work", [P, NB, 4, BLK])
        wa = sb("wa", [P, 4, D])
        va = sb("va", [P, VA])
        wo = sb("wo", [P, D])
        w1 = sb("w1", [P, FF])
        w2 = sb("w2", [P, FT, D])
        vd = sb("vd", [P, VD])
        rows = sb("rows", [P, 2, D])
        context_raw = sb("context_raw", [P, NB, BLK])
        context = sb("context", [P, QT, NH, DH])
        rden = sb("rden", [P, TB, G])
        top = sb("top", [P, 2, G, QT])
        top2 = sb("top2", [P, 2, G, QT])
        neg_top = sb("neg_top", [G * QT, 2, 2, P], BF16)
        stats = sb("stats", [P, NT, 6])
        moments = sb("moments", [P, NT, 2])
        var = sb("var", [P, NT])
        rstd = sb("rstd", [P, NT])
        newton = sb("newton", [P, NT])
        ident = sb("ident", [P, P])
        ident_b = sb("ident_b", [P, P], BF16)
        mask_b = sb("mask_b", [P, P], BF16)
        acc = sb("acc", [P, NT, D])
        we = sb("we", [P, 2, 2 * FF])
        be = sb("be", [P, EXPERTS, FT])
        b1_now = sb("b1_now", [P, 2, FT])
        gate_now = sb("gate_now", [P, 2, NT])
        wr = sb("wr", [P, E])
        b2_rows = sb("b2_rows", [EXPERTS, D])
        logit = sb("logit", [P, NT, E])
        prob_e = sb("prob_e", [P, NT, E])
        rank = sb("rank", [P, NT, E])
        cmp = sb("cmp", [P, NT, E])
        one_col = sb("one_col", [P, NT])
        gates = sb("gates", [P, NT, EXPERTS])
        gates_e = sb("gates_e", [P, EXPERTS, NT])
        flat = work[:, :, :, :].rearrange("p a b c -> p (a b c)")
        x2_t = flat[:, 0:NT * P]
        gates_t = flat[0:EXPERTS, NT * P:2 * NT * P]

        def bank(name):
            return ctx.enter_context(nc.psum_tensor(name, [P, 512], F32))

        bank_max = [bank("bank_max0"), bank("bank_max1")]
        bank_score = [bank("bank_score0"), bank("bank_score1")]
        bank_pv = [bank("bank_pv0"), bank("bank_pv1")]
        bank_small = bank("bank_small")
        bank_proj = bank("bank_proj")
        proj = [bank_max[0], bank_max[1], bank_proj]

        const_in = sem("const_in")
        x_in = sem("x_in")
        wa_in, wd_in = sem("wa_in"), sem("wd_in")
        stack_in = [sem(f"stack_in{s}") for s in range(NQ)]
        shift_in = [sem(f"shift_in{s}") for s in range(NQ)]
        split_out = sem("split_out")
        init_done = sem("init_done")
        passed = sem("passed")
        score_ready = sem("score_ready")
        exp_done = sem("exp_done")
        mask_done = sem("mask_done")
        pv_done = sem("pv_done")
        pv_read = sem("pv_read")
        max_ready = sem("max_ready")
        max_done = sem("max_done")
        merged = sem("merged")
        small_ready = sem("small_ready")
        small_read = sem("small_read")
        neg_done = sem("neg_done")
        rden_done = sem("rden_done")
        bias_sum = sem("bias_sum")
        a_ready, a_act, a_dve = sem("a_ready"), sem("a_act"), sem("a_dve")
        a_turned, a_split, a_pool = sem("a_turned"), sem("a_split"), sem("a_pool")
        a_normed, d_normed = sem("a_normed"), sem("d_normed")
        d_ready, d_act, d_dve = sem("d_ready"), sem("d_act"), sem("d_dve")
        bias_added = sem("bias_added")
        ln_a, ln_d, ln_x = sem("ln_a"), sem("ln_d"), sem("ln_x")
        x_normed = sem("x_normed")
        xt_ready, xt_read = sem("xt_ready"), sem("xt_read")
        router_done, router = sem("router_done"), sem("router")
        router_exp = sem("router_exp")
        gates_ready, gates_read = sem("gates_ready"), sem("gates_read")
        b2_ready, b2_read = sem("b2_ready"), sem("b2_read")
        we_in = [sem("we_in0"), sem("we_in1")]
        up_ready, gelu_done = sem("up_ready"), sem("gelu_done")
        down_ready, acc_done = sem("down_ready"), sem("acc_done")
        gate_copied = sem("gate_copied")
        finished, out_done = sem("finished"), sem("out_done")

        def n_score(q, u, g):
            return (q * NU + u) * G + g + 1

        def n_exp(q, u, g):
            return (q * NU + u) * G + g + 1 + 2

        def n_mask(q, u):
            return q * len(MASKED) + MASKED.index(u) + 1

        def n_pv(q, u):
            return q * NU + u + 1 + RING

        def n_pv_read(q, b):
            return q * NB + b + 1 + NB

        def n_max(v, g):
            return v * G + g + 1

        def n_max_done(v, g):
            return v * G + g + 1 + 2

        def n_small(q, k):
            return q * 3 + k + 4

        def load_stacks(sp, H, s):
            b = H[1]
            ch = slice(s * G * DH, (s + 1) * G * DH)
            for i in range(NP):
                for part, what, dst, row in ((Q_PARTS[i], 0, q_stack, 0), (Q_PARTS[i], 1, q_stack, REL),
                                             (K_PARTS[i], 2, k_stack, 0)):
                    r0 = row + i * DH
                    sp.dma_start(dst[r0:r0 + DH, s, :, :],
                                 scratch[b, part, what, ch, :].rearrange("(g d) t -> d g t", d=DH))\
                      .then_inc(stack_in[s], 16)

        N_STACK = 16 * 3 * NP

        def load_shift(sp, q, s, par):
            sp.wait_ge(neg_done, q * 2 + 2)
            for i in range(2):
                sp.dma_start(q_stack[SHIFT + i:SHIFT + i + 1, s, :, :].rearrange("o g (t c) -> o (g t) c", c=P),
                             neg_top[:, par, i, :]).then_inc(shift_in[s], 16)

        def store_split(sp, H):
            if not isinstance(H[0], int) or H[0] > 0:
                for s in range(NQ):
                    sp.wait_ge(stack_in[s], (H[0] - 1) * N_STACK + 16)
            for n in range(NB):
                for what, ready in ((0, 0), (1, 2), (2, 1)):
                    sp.wait_ge(a_pool, H[0] * A_POOL + 7 * n + 5 + ready + 1)
                    sp.dma_start(scratch[H[1], :, what, :, n * BLK:(n + 1) * BLK].rearrange("a c t -> c a t"),
                                 split[:, n, :, what, :]).then_inc(split_out, 16)
            sp.wait_ge(split_out, (H[0] + 1) * (16 * 3 * NB) + 16)

        def load_a_weights(sp, l):
            if isinstance(l, int):
                w, v = wa_d[l], va_d[l]
            else:
                w = wa_d[bass.ds(l, 1)].rearrange("o p n -> (o p) n")
                v = va_d[bass.ds(l, 1)].rearrange("o p n -> (o p) n")
            sp.dma_start(wa[:, :, :].rearrange("p a n -> p (a n)"), w).then_inc(wa_in, 16)
            sp.dma_start(va[:, 0:VA - 1], v).then_inc(wa_in, 16)

        def load_d_weights(sp, l):
            if isinstance(l, int):
                w, v, r = wd_d[l], vd_d[l], rows_d[l:l + 1]
            else:
                w = wd_d[bass.ds(l, 1)].rearrange("o p n -> (o p) n")
                v = vd_d[bass.ds(l, 1)].rearrange("o p n -> (o p) n")
                r = rows_d[bass.ds(l, 1)]
            sp.dma_start(wo[:, :], w[:, 0:D]).then_inc(wd_in, 16)
            sp.dma_start(w1[:, :], w[:, D:D + FF]).then_inc(wd_in, 16)
            sp.dma_start(w2[:, :, :].rearrange("p a n -> p (a n)"), w[:, D + FF:D + 2 * FF]).then_inc(wd_in, 16)
            sp.dma_start(vd[:, :], v).then_inc(wd_in, 16)
            sp.dma_start(rows[:, :, :].rearrange("p a n -> p (a n)"), r.broadcast_to((P, 2 * D)))\
              .then_inc(wd_in, 16)

        N_WA, N_WD = 32, 80

        def sp_half(sp, H, b, more=True, reload=True):
            nxt = (H + 1, 1 - b)
            load_shift(sp, H * NQ + 1, 1, 1)
            load_shift(sp, H * NQ + 2, 2, 0)
            if more:
                store_split(sp, nxt)
                for s in range(2):
                    sp.wait_ge(score_ready, n_score(H * NQ + s, NU - 1, G - 1))
                    load_stacks(sp, nxt, s)
            load_shift(sp, H * NQ + 3, 3, 1)
            if more:
                sp.wait_ge(score_ready, n_score(H * NQ + 2, NU - 1, G - 1))
                load_stacks(sp, nxt, 2)
                load_shift(sp, H * NQ + 4, 0, 0)
                sp.wait_ge(score_ready, n_score(H * NQ + 3, NU - 1, G - 1))
                load_stacks(sp, nxt, 3)
            if more and reload and b == 0:
                for done, count in ((a_act, A_ACT), (a_dve, A_DVE), (a_ready, A_USES)):
                    sp.wait_ge(done, (H + 2) * count)
                    sp.sem_inc(passed, 1)
                load_a_weights(sp, layer_of(H) + 1)
            if more and b == 1:
                for done, count in ((d_dve, D_DVE), (d_act, D_ACT), (bias_added, 2)):
                    sp.wait_ge(done, (H + 1) * count)
                    sp.sem_inc(passed, 1)
                load_d_weights(sp, layer_of(H) + 1)

        layer_reg = {}

        def layer_of(H):
            return H // 2 if isinstance(H, int) else layer_reg[0]

        def statistics(dve, chain, base, src, t0, n, eps):
            for t in range(n):
                nc.vector.bn_stats(stats[:, t, :], src[:, t0 + t, :]).then_inc(chain, 1)
            dve.wait_ge(chain, base + n)
            dve.sem_inc(passed, 1)
            for t in range(n):
                nc.vector.bn_aggr(moments[:, t, :], stats[:, t, :]).then_inc(chain, 1)
            dve.wait_ge(chain, base + 2 * n)
            k = 2 * n
            nc.vector.tensor_scalar(var[:, 0:n], moments[:, 0:n, 1], float(eps), None, ALU.add).then_inc(chain, 1)
            k += 1
            dve.wait_ge(chain, base + k)
            nc.vector.tensor_scalar(newton[:, 0:n].bitcast(I32), var[:, 0:n].bitcast(I32), 1, None,
                                    ALU.logical_shift_right).then_inc(chain, 1)
            k += 1
            dve.wait_ge(chain, base + k)
            nc.vector.tensor_scalar(rstd[:, 0:n].bitcast(I32), newton[:, 0:n].bitcast(I32), -1.0,
                                    float(0x5f3759df), ALU.mult, ALU.add).then_inc(chain, 1)
            k += 1
            for _ in range(NEWTON):
                dve.wait_ge(chain, base + k)
                nc.vector.tensor_tensor(newton[:, 0:n], rstd[:, 0:n], rstd[:, 0:n], ALU.mult).then_inc(chain, 1)
                dve.wait_ge(chain, base + k + 1)
                nc.vector.tensor_tensor(newton[:, 0:n], newton[:, 0:n], var[:, 0:n], ALU.mult).then_inc(chain, 1)
                dve.wait_ge(chain, base + k + 2)
                nc.vector.tensor_scalar(newton[:, 0:n], newton[:, 0:n], -0.5, 1.5, ALU.mult, ALU.add)\
                  .then_inc(chain, 1)
                dve.wait_ge(chain, base + k + 3)
                nc.vector.tensor_tensor(rstd[:, 0:n], rstd[:, 0:n], newton[:, 0:n], ALU.mult).then_inc(chain, 1)
                k += 4
            dve.wait_ge(chain, base + k)

        def centre(dst, src, t, ts):
            return nc.vector.tensor_scalar(dst[:, t, :], src[:, ts, :], moments[:, t, 0:1], rstd[:, t:t + 1],
                                           ALU.subtract, ALU.mult)

        def a_dve_part(dve, H, b):
            statistics(dve, ln_a, H * LN_OPS, h, b * QT, QT, EPS_LAYER)
            for t in range(QT):
                last = centre(centred, h, t, b * QT + t)
                if t % TB == TB - 1:
                    last.then_inc(a_normed, 1)
            dve.wait_ge(wa_in, (layer_of_next[0] + 1) * N_WA)
            nc.vector.tensor_tensor(va[:, 7:8], va[:, 3:4], va[:, 4:5], ALU.add).then_inc(bias_sum, 1)
            dve.wait_ge(bias_sum, H + 1)
            dve.wait_ge(a_pool, H * A_POOL + 1)
            for n in range(NB):
                tok = slice(n * BLK, (n + 1) * BLK)
                dve.wait_ge(a_act, H * A_ACT + 4 * n + 2)
                nc.vector.scalar_tensor_tensor(work[:, n, 2, :], work[:, n, 0, :], va[:, 2:3], rot[:, 0, tok],
                                               ALU.add, ALU.mult).then_inc(a_turned, 1)
                dve.wait_ge(a_ready, H * A_USES + 5 * n + 3)
                nc.vector.scalar_tensor_tensor(work[:, n, 3, :], proj[(5 * n + 2) % 3][:, :], va[:, 7:8],
                                               rot[:, 1, tok], ALU.add, ALU.mult).then_inc(a_dve, 1)

        def a_pe_part(pe, H, b, layer, v_last=None):
            def free(k):
                if k < 3:
                    return
                kk = k - 3
                n, j = divmod(kk, 5)
                if j == 2:
                    pe.wait_ge(a_dve, H * A_DVE + n + 1)
                else:
                    pe.wait_ge(a_act, H * A_ACT + 4 * n + (1, 2, 0, 3, 4)[j])

            if v_last is not None:
                pe.wait_ge(max_done, n_max_done(v_last, G - 1))
            pe.wait_ge(wa_in, (layer + 1) * N_WA)
            for n in range(NB):
                k = 5 * n
                pe.wait_ge(a_normed, H * NB + n + 1)
                free(k)
                for t in range(TB):
                    last = nc.tensor.transpose(proj[k % 3][:, t * P:(t + 1) * P], centred[:, n * TB + t, :],
                                               ident[:, :])
                last.then_inc(a_ready, 1)
                pe.wait_ge(a_act, H * A_ACT + 4 * n + 1)
                for j, w in ((1, 0), (2, 1), (3, 2)):
                    free(k + j)
                    nc.tensor.matmul(proj[(k + j) % 3][:, :], wa[:, w, :], xn_t[:, n * BLK:(n + 1) * BLK],
                                     start=True, stop=True).then_inc(a_ready, 1)
                free(k + 4)
                for t in range(TB):
                    tt = n * TB + t
                    last = nc.tensor.matmul(proj[(k + 4) % 3][:, t * P:(t + 1) * P], xn_t[:, tt * P:(tt + 1) * P],
                                            wa[:, 3, :], start=True, stop=True)
                last.then_inc(a_ready, 1)
            pe.wait_ge(a_act, (H + 1) * A_ACT)
            pe.wait_ge(a_dve, (H + 1) * A_DVE)

        def a_act_part(act, H, b, layer):
            act.wait_ge(wa_in, (layer + 1) * N_WA)
            act.wait_ge(a_pool, H * A_POOL + 1)
            for n in range(NB):
                k = 5 * n
                act.wait_ge(a_ready, H * A_USES + k + 1)
                nc.scalar.activation(xn_t[:, n * BLK:(n + 1) * BLK], proj[k % 3][:, :], ACT.Identity,
                                     bias=va[:, 6:7], scale=va[:, 5:6]).then_inc(a_act, 1)
                for j, slot, col in ((1, 0, 0), (3, 1, 1)):
                    act.wait_ge(a_ready, H * A_USES + k + j + 1)
                    nc.scalar.activation(work[:, n, slot, :], proj[(k + j) % 3][:, :], ACT.Identity,
                                         bias=va[:, col:col + 1]).then_inc(a_act, 1)
                act.wait_ge(a_ready, H * A_USES + k + 5)
                nc.scalar.activation(values[:, b, n * TB:(n + 1) * TB, :, 0:DH],
                                     proj[(k + 4) % 3][:, :].rearrange("p (t h d) -> p t h d", t=TB, d=DH),
                                     ACT.Copy).then_inc(a_act, 1)
                if n == 0:
                    act.wait_ge(split_out, H * (16 * 3 * NB) + 16)
                base = H * A_SPLIT + 6 * n
                pool = H * A_POOL + 7 * n + 1
                act.wait_ge(a_act, H * A_ACT + 4 * n + 3)
                for what, src in ((0, 0), (2, 1), (1, 2)):
                    if what == 1:
                        act.wait_ge(a_pool, pool + 1)
                    nc.scalar.activation(split[:, n, 0, what, :], work[:, n, src, :], ACT.Copy).then_inc(a_split, 1)
                for i, (what, src) in enumerate(((0, 0), (2, 1), (1, 2))):
                    act.wait_ge(a_pool, pool + 2 + i)
                    nc.scalar.activation(split[:, n, 1, what, :], work[:, n, src, :], ACT.Copy).then_inc(a_split, 1)

        def a_pool_part(pool, H, b):
            for n in range(NB):
                act_n = H * A_SPLIT + 6 * n
                pool.wait_ge(a_turned, H * NB + n + 1)
                pool.wait_ge(a_dve, H * A_DVE + n + 1)
                nc.gpsimd.tensor_tensor(work[:, n, 2, :], work[:, n, 2, :], work[:, n, 3, :], ALU.add)\
                  .then_inc(a_pool, 1)
                for i, (what, src) in enumerate(((0, 0), (2, 1), (1, 2))):
                    pool.wait_ge(a_split, act_n + i + 1)
                    nc.gpsimd.tensor_tensor(work[:, n, src, :], work[:, n, src, :], split[:, n, 0, what, :],
                                            ALU.subtract).then_inc(a_pool, 1)
                for i, (what, src) in enumerate(((0, 0), (2, 1), (1, 2))):
                    pool.wait_ge(a_split, act_n + 3 + i + 1)
                    nc.gpsimd.tensor_tensor(split[:, n, 2, what, :], work[:, n, src, :], split[:, n, 1, what, :],
                                            ALU.subtract).then_inc(a_pool, 1)

        def d_pe_part(pe, H, b, layer, v_last, n_context):
            act_uses = {0: 1, 1: 2, 4: 3, 5: 4} | {6 + i: 5 + i for i in range(8)}
            dve_uses = {2: 1, 3: 2}

            def free(k):
                if k < 3:
                    return
                kk = k - 3
                if kk in act_uses:
                    pe.wait_ge(d_act, H * D_ACT + act_uses[kk])
                else:
                    pe.wait_ge(d_dve, H * D_DVE + dve_uses[kk])

            pe.wait_ge(small_read, n_context)
            pe.wait_ge(max_done, n_max_done(v_last, G - 1))
            pe.wait_ge(wd_in, (layer + 1) * N_WD)
            for n in range(NB):
                for t in range(TB):
                    last = nc.tensor.transpose(proj[n][:, t * P:(t + 1) * P],
                                               context[:, n * TB + t, :, :].rearrange("p h d -> p (h d)"),
                                               ident[:, :])
                last.then_inc(d_ready, 1)
            for n in range(NB):
                free(2 + n)
                pe.wait_ge(d_act, H * D_ACT + n + 1)
                for t in range(TB):
                    tt = n * TB + t
                    last = nc.tensor.matmul(proj[(2 + n) % 3][:, t * P:(t + 1) * P], d_t[:, tt * P:(tt + 1) * P],
                                            wo[:, :], start=True, stop=True)
                last.then_inc(d_ready, 1)
            for n in range(NB):
                pe.wait_ge(d_normed, H * NB + n + 1)
                free(4 + n)
                for t in range(TB):
                    last = nc.tensor.transpose(proj[(4 + n) % 3][:, t * P:(t + 1) * P], centred[:, n * TB + t, :],
                                               ident[:, :])
                last.then_inc(d_ready, 1)
            for n in range(NB):
                pe.wait_ge(d_act, H * D_ACT + 3 + n)
                for f in range(FT):
                    k = 6 + n * FT + f
                    free(k)
                    nc.tensor.matmul(proj[k % 3][:, :], w1[:, f * P:(f + 1) * P], d_t[:, n * BLK:(n + 1) * BLK],
                                     start=True, stop=True).then_inc(d_ready, 1)
            for n in range(NB):
                free(14 + n)
                pe.wait_ge(d_act, H * D_ACT + 4 + FT * (n + 1))
                for t in range(TB):
                    for f in range(FT):
                        last = nc.tensor.matmul(proj[(n + 14) % 3][:, t * P:(t + 1) * P],
                                                probs[:, n, f, t * P:(t + 1) * P], w2[:, f, :],
                                                start=f == 0, stop=f == FT - 1)
                last.then_inc(d_ready, 1)
            pe.wait_ge(d_act, (H + 1) * D_ACT)
            pe.wait_ge(d_dve, (H + 1) * D_DVE)

        D_ALL = D_USES + 2

        def d_act_part(act, H, b, layer):
            act.wait_ge(wd_in, (layer + 1) * N_WD)
            for n in range(NB):
                act.wait_ge(d_ready, H * D_ALL + n + 1)
                nc.scalar.activation(d_t[:, n * BLK:(n + 1) * BLK], proj[n][:, :], ACT.Identity, bias=vd[:, 0:1])\
                  .then_inc(d_act, 1)
            for n in range(NB):
                act.wait_ge(d_ready, H * D_ALL + 5 + n)
                nc.scalar.activation(d_t[:, n * BLK:(n + 1) * BLK], proj[(4 + n) % 3][:, :], ACT.Identity,
                                     bias=vd[:, 2:3], scale=vd[:, 1:2]).then_inc(d_act, 1)
            for n in range(NB):
                for f in range(FT):
                    k = 6 + n * FT + f
                    act.wait_ge(d_ready, H * D_ALL + k + 1)
                    nc.scalar.activation(probs[:, n, f, :], proj[k % 3][:, :], ACT.Gelu, bias=vd[:, 3 + f:4 + f])\
                      .then_inc(d_act, 1)

        def d_dve_part(dve, H, b):
            def add_in(n, use):
                dst = h[:, b * QT + n * TB:b * QT + (n + 1) * TB, :]
                nc.vector.tensor_tensor(dst, dst, proj[use % 3][:, :].rearrange("p (t c) -> p t c", t=TB), ALU.add)\
                  .then_inc(d_dve, 1)

            dve.wait_ge(bias_added, 2 * H + 1)
            for n in range(NB):
                dve.wait_ge(d_ready, H * D_ALL + 3 + n)
                add_in(n, 2 + n)
            dve.wait_ge(d_dve, H * D_DVE + NB)
            statistics(dve, ln_d, H * LN_OPS, h, b * QT, QT, EPS_LAYER)
            for t in range(QT):
                last = centre(centred, h, t, b * QT + t)
                if t % TB == TB - 1:
                    last.then_inc(d_normed, 1)
            dve.wait_ge(bias_added, 2 * H + 2)
            for n in range(NB):
                dve.wait_ge(d_ready, H * D_ALL + D_USES + n + 1)
                add_in(n, 14 + n)
            dve.wait_ge(d_dve, (H + 1) * D_DVE)

        def add_row(pool, b, i):
            dst = h[:, b * QT:(b + 1) * QT, :]
            nc.gpsimd.tensor_tensor(dst, dst, rows[:, i:i + 1, :].broadcast_to((P, QT, D)), ALU.add)\
              .then_inc(bias_added, 1)

        def slot_of(v_rel):
            quad, c = divmod(v_rel, NU)
            return quad % NQ, quad % 2, c

        def pe_pass1(pe, H, v_rel):
            s, par, c = slot_of(v_rel)
            qt, k0, n = CHUNKS[c]
            v = H * (NQ * NU) + v_rel
            if c == 0:
                pe.wait_ge(stack_in[s], (H + v_rel // NU // NQ + 1) * N_STACK + 16)
            return [(g, qt, k0, n, v, s) for g in range(G)]

        def pe_pass1_one(pe, item):
            g, qt, k0, n, v, s = item
            pe.wait_ge(max_done, n_max_done(v, g) - 2)
            has_diagonal = k0 + n == (qt + 1) * P
            mm = nc.tensor.matmul(bank_max[g % 2][:, 0:n], q_stack[0:SHIFT, s, g, qt * P:(qt + 1) * P],
                                  k_stack[0:SHIFT, s, g, k0:k0 + n], start=True, stop=not has_diagonal)
            if has_diagonal:
                mm = nc.tensor.matmul(bank_max[g % 2][:, n - P:n], ident_b[:, :], mask_b[:, :],
                                      start=False, stop=True)
            mm.then_inc(max_ready, 1)

        def dve_pass1(dve, H, v_rel):
            s, par, c = slot_of(v_rel)
            qt, k0, n = CHUNKS[c]
            v = H * (NQ * NU) + v_rel
            dst = top if k0 == 0 else top2
            for g in range(G):
                dve.wait_ge(max_ready, n_max(v, g))
                nc.vector.reduce_max(dst[:, par, g, qt:qt + 1], bank_max[g % 2][:, 0:n], AX.X).then_inc(max_done, 1)
            if c == NU - 1:
                dve.wait_ge(max_done, n_max_done(v, G - 1))
                nc.vector.tensor_tensor(top[:, par, :, TB:QT], top[:, par, :, TB:QT], top2[:, par, :, TB:QT], ALU.max)\
                  .then_inc(merged, 1)

        def pe_top(pe, q, par, small):
            pe.wait_ge(merged, q + 1)
            if small is not None:
                pe.wait_ge(small_read, small - 1)
            nc.tensor.transpose(bank_small[0:G * QT, 0:P], top[:, par, :, :].rearrange("p g t -> p (g t)"),
                                ident[:, :]).then_inc(small_ready, 1)

        def dve_top(dve, q, par, s, small):
            dve.wait_ge(small_ready, small)
            if q is not None:
                dve.wait_ge(neg_done, q * 2)
            dst = neg_top[:, par, :, :]
            nc.vector.tensor_scalar(dst[:, 0, :], bank_small[0:G * QT, 0:P], -1.0, None, ALU.mult).then_inc(neg_done, 1)
            qq = 0 if q is None else q
            dve.wait_ge(neg_done, qq * 2 + 1)
            nc.vector.scalar_tensor_tensor(dst[:, 1, :], bank_small[0:G * QT, 0:P], -1.0, dst[:, 0, :], ALU.mult,
                                           ALU.subtract).then_inc(neg_done, 1)
            dve.wait_ge(neg_done, qq * 2 + 2)
            dve.sem_inc(small_read, 1)

        def pe_scores(pe, H, s, u):
            b, t = UNITS[u]
            first, n = span(u)
            q = H * NQ + s
            if u == 0:
                pe.wait_ge(shift_in[s], (H + 1) * 32 + (16 if s == NQ - 1 else 0))
            return [(q, s, u, g, t, b * BLK + first, n) for g in range(G)]

        def pe_score_one(pe, item):
            q, s, u, g, t, q0, n = item
            pe.wait_ge(exp_done, n_exp(q, u, g) - 2)
            nc.tensor.matmul(bank_score[g % 2][:, 0:n], k_stack[0:ROWS, s, g, t * P:(t + 1) * P],
                             q_stack[0:ROWS, s, g, q0:q0 + n], start=True, stop=True).then_inc(score_ready, 1)

        def act_exps(act, H, s, u):
            first, n = span(u)
            q = H * NQ + s
            act.wait_ge(pv_done, n_pv(q, u) - RING)
            for g in range(G):
                act.wait_ge(score_ready, n_score(q, u, g))
                nc.scalar.activation(probs[:, u % RING, g, 0:n], bank_score[g % 2][:, 0:n], ACT.Exp, scale=SCALE)\
                  .then_inc(exp_done, 1)

        def pool_mask(pool, H, s, u):
            q = H * NQ + s
            pool.wait_ge(exp_done, n_exp(q, u, G - 1))
            pool.sem_inc(passed, 1)
            tile = probs[:, u % RING, :, 0:P]
            nc.gpsimd.affine_select(out=tile, in_=tile, compare_op=ALU.is_ge, fill=0.0, base=0,
                                    pattern=[[0, G], [1, P]], channel_multiplier=-1).then_inc(mask_done, 1)

        def pe_pv(pe, H, b, s, u):
            blk, t = UNITS[u]
            first, n = span(u)
            q = H * NQ + s
            if diagonal(u):
                pe.wait_ge(mask_done, n_mask(q, u))
            else:
                pe.wait_ge(exp_done, n_exp(q, u, G - 1))
            if t == 0:
                pe.wait_ge(pv_read, n_pv_read(q - 1, blk))
            for g in range(G):
                last = nc.tensor.matmul(bank_pv[blk][32 * g:32 * g + V_COLS, first:first + n],
                                        values[:, b, t, s * G + g, :], probs[:, u % RING, g, 0:n],
                                        start=t == 0, stop=t == TB * (blk + 1) - 1)
            last.then_inc(pv_done, 1)

        def act_pv_out(act, H, s, blk):
            q = H * NQ + s
            u = UNITS.index((blk, TB * (blk + 1) - 1))
            act.wait_ge(pv_done, n_pv(q, u))
            act.wait_ge(small_ready, n_small(q - 1, 2 * blk))
            nc.scalar.activation(context_raw[:, blk, :], bank_pv[blk][:, :], ACT.Copy).then_inc(pv_read, 1)

        def pe_tail(pe, H, s, blk, before):
            q = H * NQ + s
            pe.wait_ge(pv_read, n_pv_read(q, blk))
            pe.wait_ge(small_read, before)
            for t in range(TB):
                last = nc.tensor.transpose(bank_small[:, t * P:(t + 1) * P], context_raw[:, blk, t * P:(t + 1) * P],
                                           ident[:, :])
            last.then_inc(small_ready, 1)

        def dve_tail(dve, H, s, blk, ready):
            q = H * NQ + s
            dve.wait_ge(small_ready, ready)
            got = bank_small[:, :].rearrange("p (t g c) -> p t g c", t=TB, g=G)
            nc.vector.reciprocal(rden[:, :, :], got[:, :, :, DH]).then_inc(rden_done, 1)
            dve.wait_ge(rden_done, q * NB + blk + 1)
            nc.vector.tensor_tensor(context[:, blk * TB:(blk + 1) * TB, s * G:(s + 1) * G, :], got[:, :, :, 0:DH],
                                    rden[:, :, :].unsqueeze(3).broadcast_to((P, TB, G, DH)), ALU.mult)\
              .then_inc(small_read, 1)

        RAW0, TAIL0, TOP, RAW1, TAIL1 = 6, 8, 9, 2, 4

        def steps(H, b, more, on_unit, on_end, on_a, on_d):
            for run in range(2):
                for s in (2 * run, 2 * run + 1):
                    for u in range(NU):
                        on_unit(run, s, u)
                on_end(run)
                if run == 0:
                    if more:
                        on_a()
                else:
                    on_d()

        def v_exists(more, v_rel):
            return more or v_rel < NQ * NU

        def last_v(more, s):
            v = s * NU + NU - 1 + AHEAD
            return v if more else min(v, NQ * NU - 1)

        def pe_half(pe, H, b, layer, more=True):
            def small(s, k):
                n = n_small(H * NQ + s, k)
                return n if more or s < NQ - 1 or k == 0 else n - 1

            def on_unit(run, s, u):
                scores = pe_scores(pe, H, s, u)
                v_rel = s * NU + u + AHEAD
                maxes = pe_pass1(pe, H, v_rel) if v_exists(more, v_rel) else [None] * G
                for a, m in zip(scores, maxes):
                    pe_score_one(pe, a)
                    if m:
                        pe_pass1_one(pe, m)
                first_of_run = s % 2 == 0
                if not (first_of_run and u < LAG):
                    pe_pv(pe, H, b, s if u >= LAG else s - 1, (u - LAG) % NU)
                if u == TAIL0:
                    pe_tail(pe, H, s, 0, small(s, 0) - 1)
                if u == TOP and (more or s < NQ - 1):
                    pe_top(pe, H * NQ + s + 1, (s + 1) % 2, small(s, 1))
                if u == TAIL1 and not first_of_run:
                    pe_tail(pe, H, s - 1, 1, small(s - 1, 2) - 1)

            def on_end(run):
                s = 2 * run + 1
                for u in range(NU - LAG, NU):
                    pe_pv(pe, H, b, s, u)
                pe_tail(pe, H, s, 1, small(s, 2) - 1)

            steps(H, b, more, on_unit, on_end,
                  lambda: a_pe_part(pe, H + 1, 1 - b, layer if b == 0 else layer + 1,
                                    H * (NQ * NU) + last_v(more, 1)),
                  lambda: d_pe_part(pe, H, b, layer, H * (NQ * NU) + last_v(more, NQ - 1), small(NQ - 1, 2)))

        def act_half(act, H, b, layer, more=True):
            def on_unit(run, s, u):
                act_exps(act, H, s, u)
                if u == RAW0:
                    act_pv_out(act, H, s, 0)
                if u == RAW1 and s % 2:
                    act_pv_out(act, H, s - 1, 1)

            steps(H, b, more, on_unit, lambda run: act_pv_out(act, H, 2 * run + 1, 1),
                  lambda: a_act_part(act, H + 1, 1 - b, layer if b == 0 else layer + 1),
                  lambda: d_act_part(act, H, b, layer))

        layer_of_next = {}

        def dve_half(dve, H, b, layer, more=True):
            def small(s, k):
                n = n_small(H * NQ + s, k)
                return n if more or s < NQ - 1 or k == 0 else n - 1

            def on_unit(run, s, u):
                v_rel = s * NU + u + AHEAD
                if v_exists(more, v_rel):
                    dve_pass1(dve, H, v_rel)
                if u == TAIL0:
                    dve_tail(dve, H, s, 0, small(s, 0))
                if u == TOP and (more or s < NQ - 1):
                    nq = H * NQ + s + 1
                    dve.wait_ge(shift_in[(s - 1) % NQ], (H + 1) * 32 if s > 0 else H * 32 + 16)
                    dve_top(dve, nq, (s + 1) % 2, (s + 1) % NQ, small(s, 1))
                if u == TAIL1 and s % 2:
                    dve_tail(dve, H, s - 1, 1, small(s - 1, 2))

            def on_a():
                layer_of_next[0] = layer if b == 0 else layer + 1
                a_dve_part(dve, H + 1, 1 - b)

            steps(H, b, more, on_unit, lambda run: dve_tail(dve, H, 2 * run + 1, 1, small(2 * run + 1, 2)),
                  on_a, lambda: d_dve_part(dve, H, b))

        def pool_half(pool, H, b, layer, more=True):
            def on_unit(run, s, u):
                if diagonal(u):
                    pool_mask(pool, H, s, u)
                if s == 0 and u == NU - 1:
                    pool.wait_ge(wd_in, (layer + 1) * N_WD)
                    add_row(pool, b, 0)

            def on_d():
                pool.wait_ge(d_normed, H * NB + NB)
                add_row(pool, b, 1)

            steps(H, b, more, on_unit, lambda run: None, lambda: a_pool_part(pool, H + 1, 1 - b), on_d)

        def run_halves(eng, half):
            with eng.Fori(0, L - 1) as l:
                layer_reg[0] = l
                half(eng, l * 2, 0, l)
                half(eng, l * 2 + 1, 1, l)
            half(eng, 2 * L - 2, 0, L - 1)
            half(eng, 2 * L - 1, 1, L - 1, False)

        INIT = 5
        ROUTER_STEPS = 5 + 3 * E + 3
        N_CONST = 16 * (7 + NQ * G)
        WE = 2 * FF

        up_banks = [bank_score[0], bank_score[1], bank_max[0], bank_max[1]]
        down_banks = bank_pv

        block = ctx.enter_context(nc.Block())

        @block.sync
        def _(sp):
            xv = x_d.rearrange("b (t p) c -> p (b t) c", p=P)
            sp.dma_start(h[:, :, :], xv).then_inc(x_in, 16)
            load_a_weights(sp, 0)
            sp.sem_inc(split_out, 16)
            for s in range(NQ):
                sp.sem_inc(stack_in[s], 16)
            sp.sem_inc(shift_in[NQ - 1], 16)
            for dst, src in ((ident[:, :], ident_d), (ident_b[:, :], identb_d), (mask_b[:, :], maskb_d),
                             (rot[:, :, :], rot_d), (wr[:, :], wr_d), (b2_rows[:, :], be_d[:, 0:D]),
                             (be[:, :, :], be_d[:, D:D + FF].rearrange("e (p f) -> p e f", p=P))):
                sp.dma_start(dst, src).then_inc(const_in, 16)
            for s in range(NQ):
                for g in range(G):
                    sp.dma_start(k_stack[REL:ROWS, s, g, :], kst_d).then_inc(const_in, 16)
            for e in range(2):
                sp.dma_start(we[:, e, :], we_d[e]).then_inc(we_in[e], 16)
            load_d_weights(sp, 0)
            store_split(sp, (0, 0))
            for s in range(NQ):
                load_stacks(sp, (0, 0), s)
            load_shift(sp, 0, 0, 0)

            def half(sp, H, b, layer, more=True):
                sp_half(sp, H, b, more, more and not (isinstance(H, int) and H == 2 * L - 2))

            run_halves(sp, half)
            sp.wait_ge(d_dve, 2 * L * D_DVE)
            sp.dma_start(probs[:, 0:2, :, :].rearrange("p a g n -> p (a g n)")[:, 0:NT * D]
                         .rearrange("p (t c) -> p t c", c=D), xv).then_inc(x_in, 16)
            with sp.Fori(0, E // 2 - 1) as i:
                for par in range(2):
                    sp.wait_ge(down_ready, (i * 2 + par + 1) * (NB * B) + 2)
                    sp.sem_inc(passed, 1)
                    sp.dma_start(we[:, par, :], we_d[bass.ds(i * 2 + par + 2, 1)].rearrange("o p n -> (o p) n"))\
                      .then_inc(we_in[par], 16)
            sp.wait_ge(down_ready, (E - 1) * (NB * B) + 2)
            sp.dma_start(we[:, 0, :], we_d[E]).then_inc(we_in[0], 16)
            sp.wait_ge(finished, 1)
            sp.dma_start(out_d.rearrange("b (t p) c -> p (b t) c", p=P), acc[:, :, :]).then_inc(out_done, 16)
            sp.wait_ge(out_done, 16)

        @block.gpsimd
        def _(pool):
            pool.sem_inc(a_pool, 1)
            a_pool_part(pool, 0, 0)
            run_halves(pool, pool_half)

        @block.scalar
        def _(act):
            act.sem_inc(exp_done, 2)
            act.sem_inc(pv_read, 2)
            a_act_part(act, 0, 0, 0)
            run_halves(act, act_half)
            act.sem_inc(gelu_done, 4)
            for n in range(4):
                act.wait_ge(xt_ready, n + 1)
                nc.scalar.activation(x2_t[:, n * 512:(n + 1) * 512], bank_max[n % 2][:, :], ACT.Copy)\
                  .then_inc(xt_read, 1)
            act.wait_ge(router, 2)
            nc.scalar.activation(prob_e[:, :, :], logit[:, :, :], ACT.Exp).then_inc(router_exp, 1)
            for n in range(4):
                act.wait_ge(gates_ready, n + 1)
                nc.scalar.activation(gates_t[:, n * 512:(n + 1) * 512], bank_max[n % 2][0:EXPERTS, :], ACT.Copy)\
                  .then_inc(gates_read, 1)
            for n in range(4):
                act.wait_ge(b2_ready, n + 1)
                nc.scalar.activation(acc[:, n * TB:(n + 1) * TB, :],
                                     bank_max[n % 2][:, :].rearrange("p (t c) -> p t c", t=TB), ACT.Copy)\
                  .then_inc(b2_read, 1)

            def expert(e, par, col):
                for n in range(NB * B):
                    act.wait_ge(down_ready, e * 4 + n + 1)
                    for f in range(FT):
                        act.wait_ge(up_ready, e * 16 + 4 * n + f + 1)
                        nc.scalar.activation(probs[:, 2 + n % 2, f, :], up_banks[f][:, :], ACT.Gelu_apprx_tanh,
                                             bias=b1_now[:, par, f:f + 1]).then_inc(gelu_done, 1)

            with act.Fori(0, E // 2) as i:
                for par in range(2):
                    act.wait_ge(gate_copied, i * 2 + par + 1)
                    expert(i * 2 + par, par, None)
            act.wait_ge(gate_copied, E + 1)
            expert(E, 0, None)

        @block.tensor
        def _(pe):
            pe.sem_inc(pv_done, RING)
            pe.sem_inc(small_ready, 2)
            pe.wait_ge(const_in, N_CONST)
            pe.wait_ge(init_done, INIT)
            a_pe_part(pe, 0, 0, 0)
            for v in range(AHEAD):
                for item in pe_pass1(pe, 0, v):
                    pe_pass1_one(pe, item)
                if v == NU - 1:
                    pe_top(pe, 0, 0, None)
            run_halves(pe, pe_half)
            pe.sem_inc(down_ready, 2)
            for n in range(4):
                pe.wait_ge(x_normed, n + 1)
                if n >= 2:
                    pe.wait_ge(xt_read, n - 1)
                for t in range(TB):
                    last = nc.tensor.transpose(bank_max[n % 2][:, t * P:(t + 1) * P], acc[:, n * TB + t, :],
                                               ident[:, :])
                last.then_inc(xt_ready, 1)
            pe.wait_ge(xt_read, 4)
            for t in range(NT):
                last = nc.tensor.matmul(bank_proj[:, t * E:(t + 1) * E], x2_t[:, t * P:(t + 1) * P], wr[:, :],
                                        start=True, stop=True)
            last.then_inc(router_done, 1)
            pe.wait_ge(router, ROUTER_STEPS)
            for n in range(4):
                if n >= 2:
                    pe.wait_ge(gates_read, n - 1)
                for t in range(TB):
                    last = nc.tensor.transpose(bank_max[n % 2][0:EXPERTS, t * P:(t + 1) * P],
                                               gates[:, n * TB + t, :], ident[:, :])
                last.then_inc(gates_ready, 1)
            pe.wait_ge(gates_read, 4)
            for n in range(4):
                if n >= 2:
                    pe.wait_ge(b2_read, n - 1)
                for t in range(TB):
                    tt = n * TB + t
                    last = nc.tensor.matmul(bank_max[n % 2][:, t * P:(t + 1) * P], gates_t[:, tt * P:(tt + 1) * P],
                                            b2_rows[:, :], start=True, stop=True)
                last.then_inc(b2_ready, 1)
            pe.wait_ge(b2_read, 4)

            def up(e, par, n):
                for f in range(FT):
                    pe.wait_ge(gelu_done, e * 16 + 4 * n + f + 1)
                    nc.tensor.matmul(up_banks[f][:, :], we[:, par, f * P:(f + 1) * P],
                                     x2_t[:, n * 512:(n + 1) * 512], start=True, stop=True).then_inc(up_ready, 1)

            def down(e, par, n):
                pe.wait_ge(gelu_done, e * 16 + 4 * n + FT + 4)
                pe.wait_ge(acc_done, e * 4 + n + 1)
                for t in range(TB):
                    for f in range(FT):
                        last = nc.tensor.matmul(down_banks[n % 2][:, t * P:(t + 1) * P],
                                                probs[:, 2 + n % 2, f, t * P:(t + 1) * P],
                                                we[:, par, FF + f * D:FF + (f + 1) * D],
                                                start=f == 0, stop=f == FT - 1)
                last.then_inc(down_ready, 1)

            def expert(e, par, arrived):
                pe.wait_ge(we_in[par], arrived)
                up(e, par, 0)
                for n in range(1, NB * B):
                    up(e, par, n)
                    down(e, par, n - 1)
                down(e, par, NB * B - 1)

            with pe.Fori(0, E // 2) as i:
                for par in range(2):
                    expert(i * 2 + par, par, i * 16 + 16)
            expert(E, 0, 16 * (E // 2 + 1))

        @block.vector
        def _(dve):
            nc.vector.memset(values[:, :, :, :, DH:V_COLS], 1.0).then_inc(init_done, 1)
            for b in bank_pv:
                nc.vector.memset(b[:, :], 0.0).then_inc(init_done, 1)
            nc.vector.memset(gates[:, :, E:E + 1], 1.0).then_inc(init_done, 1)
            nc.vector.memset(gates_e[:, E, :], 1.0).then_inc(init_done, 1)
            dve.sem_inc(max_done, 2)
            dve.sem_inc(small_read, 2)
            dve.wait_ge(x_in, 16)
            statistics(dve, ln_x, 0, h, 0, NT, EPS_OUT)
            n_x = LN_OPS + 2 * QT
            for t in range(NT):
                centre(h, h, t, t).then_inc(ln_x, 1)
            dve.wait_ge(ln_x, n_x + NT)
            layer_of_next[0] = 0
            dve.wait_ge(const_in, N_CONST)
            a_dve_part(dve, 0, 0)
            for v in range(AHEAD):
                dve_pass1(dve, 0, v)
                if v == NU - 1:
                    dve_top(dve, None, 0, 0, 3)
            run_halves(dve, dve_half)
            dve.wait_ge(x_in, 32)
            x_again = probs[:, 0:2, :, :].rearrange("p a g n -> p (a g n)")[:, 0:NT * D]\
                .rearrange("p (t c) -> p t c", c=D)
            nc.vector.tensor_tensor(h[:, :, :], h[:, :, :], x_again, ALU.add).then_inc(ln_x, 1)
            n_x += NT + 1
            dve.wait_ge(ln_x, n_x)
            statistics(dve, ln_x, n_x, h, 0, NT, EPS_OUT)
            for t in range(NT):
                last = centre(acc, h, t, t)
                if t % TB == TB - 1:
                    last.then_inc(x_normed, 1)
            count = [0]

            def step(ins):
                ins.then_inc(router, 1)
                count[0] += 1
                dve.wait_ge(router, count[0])

            dve.wait_ge(router_done, 1)
            got = bank_proj[:, 0:NT * E].rearrange("p (t e) -> p t e", e=E)
            step(nc.vector.tensor_reduce(one_col[:, :], got, AX.X, ALU.max))
            step(nc.vector.tensor_tensor(logit[:, :, :], got, one_col[:, :].unsqueeze(2).broadcast_to((P, NT, E)),
                                         ALU.subtract))
            dve.wait_ge(router_exp, 1)
            step(nc.vector.tensor_reduce(one_col[:, :], prob_e[:, :, :], AX.X, ALU.add))
            step(nc.vector.reciprocal(one_col[:, :], one_col[:, :]))
            step(nc.vector.tensor_tensor(prob_e[:, :, :], prob_e[:, :, :],
                                         one_col[:, :].unsqueeze(2).broadcast_to((P, NT, E)), ALU.mult))
            for o in range(E):
                other = prob_e[:, :, o:o + 1]
                last = None
                if o > 0:
                    last = nc.vector.tensor_tensor(cmp[:, :, 0:o], other.broadcast_to((P, NT, o)),
                                                   prob_e[:, :, 0:o], ALU.is_gt)
                if last is not None:
                    step(last)
                else:
                    step(nc.vector.memset(rank[:, :, :], 0.0))
                step(nc.vector.tensor_tensor(cmp[:, :, o:E], other.broadcast_to((P, NT, E - o)), prob_e[:, :, o:E],
                                             ALU.is_ge))
                step(nc.vector.tensor_tensor(rank[:, :, :], rank[:, :, :], cmp[:, :, :], ALU.add))
            step(nc.vector.tensor_scalar(cmp[:, :, :], rank[:, :, :], 2.5, None, ALU.is_lt))
            step(nc.vector.tensor_tensor(gates[:, :, 0:E], cmp[:, :, :], prob_e[:, :, :], ALU.mult))
            step(nc.vector.tensor_copy(gates_e[:, 0:E, :], gates[:, :, 0:E].rearrange("p t e -> p e t")))
            assert count[0] == ROUTER_STEPS
            dve.sem_inc(acc_done, 2)
            dve.wait_ge(b2_read, 4)

            def expert(e, par):
                for n in range(NB * B):
                    dve.wait_ge(down_ready, e * 4 + n + 3)
                    for t in range(TB):
                        tt = n * TB + t
                        last = nc.vector.scalar_tensor_tensor(acc[:, tt, :], down_banks[n % 2][:, t * P:(t + 1) * P],
                                                              gate_now[:, par, tt:tt + 1], acc[:, tt, :], ALU.mult,
                                                              ALU.add)
                    last.then_inc(acc_done, 1)

            def take_gates(e, par, at):
                nc.vector.tensor_copy(b1_now[:, par, :].unsqueeze(1), be[:, at, :])
                nc.vector.tensor_copy(gate_now[:, par, :].unsqueeze(1), gates_e[:, at, :]).then_inc(gate_copied, 1)
                dve.wait_ge(gate_copied, e + 1)

            with dve.Fori(0, E // 2) as i:
                for par in range(2):
                    e = i * 2 + par
                    take_gates(e, par, bass.ds(e, 1))
                    expert(e, par)
            take_gates(E, 0, slice(E, E + 1))
            expert(E, 0)
            dve.wait_ge(acc_done, EXPERTS * 4 + 2)
            nc.vector.scalar_tensor_tensor(acc[:, :, :], acc[:, :, :], MOE_SCALE, h[:, :, :], ALU.mult, ALU.add)\
              .then_inc(finished, 1)


def bf16_bits(a):
    b = np.ascontiguousarray(a, np.float32).view(np.uint32)
    return ((b + np.uint32(0x7fff) + ((b >> 16) & np.uint32(1))) >> 16).astype(np.uint16)


def rounded(a):
    return (bf16_bits(a).astype(np.uint32) << 16).view(np.float32)


def constants():
    half = DH // 2
    inv = (1.0 / np.float32(10000.0) ** (np.arange(0, DH, 2, dtype=np.float32) / DH)).astype(np.float32)
    angle = np.arange(S, dtype=np.float64)[None, :] * inv.astype(np.float64)[:, None]
    sin, cos = np.sin(angle), np.cos(angle)
    ch = np.arange(P) % DH
    f = ch % half
    rot = np.stack([sin[f], np.where((ch < half)[:, None], cos[f], -cos[f])], axis=1).astype(np.float32)
    table = np.concatenate([cos, sin], axis=0).astype(np.float32)
    high = rounded(table)
    middle = rounded(table - high)
    low = rounded(table - high - middle)
    parts = (high, middle, low)
    kst = np.concatenate([parts[i] for i in K_PARTS] + [np.ones((2, S), np.float32)], axis=0)
    ident = np.eye(P, dtype=np.float32)
    mask = np.where(np.arange(P)[None, :] > np.arange(P)[:, None], np.float32(NEG), np.float32(0))
    return ident, bf16_bits(ident), bf16_bits(mask), rot, bf16_bits(kst)


def kernel(**inp):
    import concourse.bacc as bacc
    from concourse.bass_utils import run_bass_kernel_spmd
    a = {k: np.asarray(v) for k, v in inp.items()}
    A = {k[8:]: v for k, v in a.items() if k.startswith("L0_attn_")}
    M = {k[7:]: v for k, v in a.items() if k.startswith("L0_ffn_")}
    swap = np.arange(P).reshape(NH, 2, DH // 2)[:, ::-1].reshape(P)
    t = lambda w: np.swapaxes(w, -1, -2)
    u = A["u_bias"].reshape(L, D)
    wa = np.concatenate([t(A["Wq"]), t(A["Wq"][:, swap]), t(A["Wk"]), t(A["Wv"])], axis=2)
    va = np.stack([A["bq"], A["bk"], u, A["bq"][:, swap], u[:, swap], A["ln1_w"], A["ln1_b"]], axis=2)
    tiles = lambda w: np.swapaxes(t(w).reshape(w.shape[0], FT, P, D), 1, 2).reshape(w.shape[0], P, FT * D)
    wd = np.concatenate([t(A["Wo"]), t(A["W1"]), tiles(A["W2"])], axis=2)
    vd = np.concatenate([np.stack([A["bv"], A["ln2_w"], A["ln2_b"]], axis=2),
                         np.swapaxes(A["b1"].reshape(L, FT, P), 1, 2), A["bv"][:, :, None]], axis=2)
    rows = np.concatenate([A["bo"], A["b2"]], axis=1)
    w1 = np.concatenate([t(M["W1"]), t(M["Ws1"])[None]], axis=0)
    w2 = np.concatenate([tiles(M["W2"]), tiles(M["Ws2"][None])], axis=0)
    we = np.concatenate([w1, w2], axis=2)
    b1 = np.concatenate([M["b1"], M["bs1"][None]], axis=0).reshape(EXPERTS, FT, P)
    b2 = np.concatenate([M["b2"], M["bs2"][None]], axis=0)
    be = np.concatenate([b2, np.swapaxes(b1, 1, 2).reshape(EXPERTS, FF)], axis=1)
    given = {"x": A["x"], "wa": wa, "va": va, "wd": wd, "vd": vd, "rows": rows, "wr": t(M["w_router"]), "we": we,
             "be": be}
    given |= dict(zip(("ident", "ident_b", "mask_b", "rot", "kst"), constants()))
    nc = bacc.Bacc("TRN2", target_bir_lowering=False, num_devices=1)
    arrays, args = {}, []
    for name, v in given.items():
        v = np.ascontiguousarray(v)
        arrays[f"in_{name}"] = v
        ap = nc.dram_tensor(f"in_{name}", v.shape, mybir.dt.from_np(v.dtype), kind="ExternalInput").ap()
        args.append(ap.bitcast(BF16) if v.dtype == np.uint16 else ap)
    args.append(nc.dram_tensor("out", (B, S, D), F32, kind="ExternalOutput").ap())
    build(nc, *args)
    r = run_bass_kernel_spmd(nc, [arrays], core_ids=[0])
    return r.results[0]["out"]
```

```python
import concourse.bass as bass
from concourse import mybir
from contextlib import ExitStack
import numpy as np

F32 = mybir.dt.float32
BF16 = mybir.dt.bfloat16
I32 = mybir.dt.int32
ALU = mybir.AluOpType
ACT = mybir.ActivationFunctionType
AX = mybir.AxisListType

B, S, D = 2, 1024, 128
L, NH, DH = 4, 16, 8
FF, E = 512, 8
P = 128
QT = S // P
BLK = 512
NB = S // BLK
TB = BLK // P
G = 4
NQ = NH // G
FT = FF // P
NT = B * QT
EXPERTS = E + 1
SCALE = float(DH) ** -0.5
MOE_SCALE = 1.0 / float(np.sqrt(1 + 2 / E))
NEG = -3.0e38
EPS_OUT, EPS_LAYER = 1e-5, 1e-6

Q_PARTS = (0, 0, 0, 1, 1, 2)
K_PARTS = (0, 1, 2, 0, 1, 0)
Q_RUNS = ((0, 3, 0), (1, 2, 0), (2, 1, 0))
K_RUNS = ((0, 3, 1), (0, 2, 1), (0, 1, 1))
NP = len(Q_PARTS)
REL = NP * DH
SHIFT = 2 * REL
ROWS = SHIFT + 2

UNITS = [(0, 0), (0, 3), (0, 1), (0, 2), (1, 0), (1, 5), (1, 1), (1, 7), (1, 2), (1, 6), (1, 3), (1, 4)]
CHUNKS = [(1, 0, 256), (3, 0, 512), (4, 0, 512), (5, 0, 512), (0, 0, 128), (2, 0, 384), (5, 512, 256),
          (6, 0, 512), (6, 512, 384), (7, 0, 512), (4, 512, 128), (7, 512, 512)]
NU = len(UNITS)
AHEAD = NU + 3
FIRST_OF = [0, 4]
LAST_OF = [3, NU - 1]
WHOLE = 256
LAG = 2
RING = 4

V_COLS = DH + 1
A_USES, A_ACT, A_DVE = 10, 8, 2
A_POOL, A_SPLIT, A_SUB = 4, 6, 3
D_USES, D_ACT, D_DVE = 16, 12, 4
NEWTON = 3
LN_OPS = 2 * QT + 2 + 4 * NEWTON
VA, VD = 8, 8

D_ROW = (4, 6)
D_CONTEXT, D_WO = (8, 9), (10, 11)
D_STATS, D_AGGR, D_NEWTON, D_CENTRE = (12, 13), 14, 15, (18, 19)
D_ROW2 = (19, 20)
D_TURN = (19, 20)
D_UP, D_GELU = (21, 25), 29
D_DOWN = ((31, 31, 31, 31), (32, 33, 34, 35))
A_STATS, A_AGGR, A_NEWTON, A_CENTRE = (36, 37), 38, 39, (42, 43)
A_BLOCK = (44, 49)
A_HIGH, A_MIDDLE = (2, 4, 4), (4, 6, 6)
A_SUBS = (3, 3, 5)
A_ADDS = (5, 5, 7, 7)
PLACES = A_BLOCK[1] + A_ADDS[-1] + 1


ORDER = np.arange(P).reshape(NQ, G, DH).transpose(0, 2, 1).reshape(P)


def diagonal(u):
    b, t = UNITS[u]
    return t >= TB * b


def span(u):
    b, t = UNITS[u]
    first = max(0, t - TB * b) * P
    return first, BLK - first


MASKED = [u for u in range(NU) if diagonal(u)]


def build(nc, x_d, wa_d, va_d, wd_d, vd_d, rows_d, wr_d, we_d, be_d, ident_d, identb_d, maskb_d, rot_d, kst_d,
          out_d):
    ctx = ExitStack()
    with ctx:
        def sb(name, shape, dt=F32):
            return ctx.enter_context(nc.sbuf_tensor(name, shape, dt))

        def sem(name):
            return ctx.enter_context(nc.semaphore(name))

        scratch = nc.dram_tensor("split_scratch", [B, 3, 3, D, S], BF16, kind="Internal").ap()

        q_stack = sb("q_stack", [P, NQ, G, S], BF16)
        k_stack = sb("k_stack", [P, NQ, G, S], BF16)
        probs = sb("probs", [P, RING, G, BLK])
        values = sb("values", [P, B, QT, NH, V_COLS])
        h = sb("h", [P, NT, D])
        xn_t = sb("xn_t", [P, S])
        d_t = sb("d_t", [P, S])
        centred = sb("centred", [P, QT, D])
        rot = sb("rot", [P, 2, S])
        split = sb("split", [P, NB, 3, 3, BLK], BF16)
        work = sb("work", [P, NB, 4, BLK])
        wa = sb("wa", [P, 4, D])
        va = sb("va", [P, VA])
        wo = sb("wo", [P, D])
        w1 = sb("w1", [P, FF])
        w2 = sb("w2", [P, FT, D])
        vd = sb("vd", [P, VD])
        rows = sb("rows", [P, 2, D])
        context_raw = sb("context_raw", [P, NB, BLK])
        context = sb("context", [P, QT, NH, DH])
        rden = sb("rden", [P, TB, G])
        top = sb("top", [P, 2, G, QT])
        top2 = sb("top2", [P, 2, G, QT])
        neg_top = sb("neg_top", [G * QT, 2, 2, P], BF16)
        stats = sb("stats", [P, NT, 6])
        moments = sb("moments", [P, NT, 2])
        var = sb("var", [P, NT])
        rstd = sb("rstd", [P, NT])
        newton = sb("newton", [P, NT])
        ident = sb("ident", [P, P])
        ident_b = sb("ident_b", [P, P], BF16)
        mask_b = sb("mask_b", [P, P], BF16)
        acc = sb("acc", [P, NT, D])
        we = sb("we", [P, 2, 2 * FF])
        inner = [acc[:, :, :].rearrange("p a b -> p (a b)").rearrange("p (f n) -> p f n", f=FT),
                 we[:, :, :].rearrange("p a b -> p (a b)").rearrange("p (f n) -> p f n", f=FT)]
        be = sb("be", [P, EXPERTS, FT])
        b1_now = sb("b1_now", [P, 2, FT])
        gate_now = sb("gate_now", [P, 2, NT])
        wr = sb("wr", [P, E])
        b2_rows = sb("b2_rows", [EXPERTS, D])
        logit = sb("logit", [P, NT, E])
        prob_e = sb("prob_e", [P, NT, E])
        rank = sb("rank", [P, NT, E])
        cmp = sb("cmp", [P, NT, E])
        one_col = sb("one_col", [P, NT])
        gates = sb("gates", [P, NT, EXPERTS])
        gates_e = sb("gates_e", [P, EXPERTS, NT])
        flat = work[:, :, :, :].rearrange("p a b c -> p (a b c)")
        x2_t = flat[:, 0:NT * P]
        gates_t = flat[0:EXPERTS, NT * P:2 * NT * P]

        def bank(name):
            return ctx.enter_context(nc.psum_tensor(name, [P, 512], F32))

        bank_max = [bank("bank_max0"), bank("bank_max1")]
        bank_score = [bank("bank_score0"), bank("bank_score1")]
        bank_pv = [bank("bank_pv0"), bank("bank_pv1")]
        bank_small = bank("bank_small")
        bank_proj = bank("bank_proj")

        const_in = sem("const_in")
        x_in = sem("x_in")
        wa_in, wd_in = sem("wa_in"), sem("wd_in")
        stack_in = [sem(f"stack_in{s}") for s in range(NQ)]
        shift_in = [sem(f"shift_in{s}") for s in range(NQ)]
        split_out = sem("split_out")
        init_done = sem("init_done")
        passed = sem("passed")
        score_ready = sem("score_ready")
        exp_done = sem("exp_done")
        mask_done = sem("mask_done")
        pv_done = sem("pv_done")
        pv_read = sem("pv_read")
        max_ready = sem("max_ready")
        max_done = sem("max_done")
        merged = sem("merged")
        small_ready = sem("small_ready")
        small_read = sem("small_read")
        neg_done = sem("neg_done")
        rden_done = sem("rden_done")
        bias_sum = sem("bias_sum")
        a_ready, a_act, a_dve_n = sem("a_ready"), sem("a_act"), sem("a_turned2")
        a_turned = sem("a_turned")
        a_split = [sem(f"a_split{n}") for n in range(NB)]
        a_sub = [sem(f"a_sub{n}") for n in range(NB)]
        a_pool = [sem(f"a_pool{n}") for n in range(NB)]
        a_normed, d_normed = sem("a_normed"), sem("d_normed")
        d_ready, d_act, d_dve = sem("d_ready"), sem("d_act"), sem("d_dve")
        d_gelu = sem("d_gelu")
        bias_added = sem("bias_added")
        ln_a, ln_d, ln_x = sem("ln_a"), sem("ln_d"), sem("ln_x")
        x_normed = sem("x_normed")
        xt_ready, xt_read = sem("xt_ready"), sem("xt_read")
        router_done, router = sem("router_done"), sem("router")
        router_exp = sem("router_exp")
        gates_ready, gates_read = sem("gates_ready"), sem("gates_read")
        b2_ready, b2_read = sem("b2_ready"), sem("b2_read")
        we_in = [sem("we_in0"), sem("we_in1")]
        up_ready, gelu_done = sem("up_ready"), sem("gelu_done")
        down_ready, acc_done = sem("down_ready"), sem("acc_done")
        gate_copied = sem("gate_copied")
        finished, out_done = sem("finished"), sem("out_done")

        def n_score(q, u, g):
            return (q * NU + u) * G + g + 1

        def n_exp(q, u, g):
            return (q * NU + u) * G + g + 1 + 2

        def n_mask(q, u):
            return q * len(MASKED) + MASKED.index(u) + 1

        def n_pv(q, u):
            return q * NU + u + 1 + RING

        def n_pv_read(q, b):
            return q * NB + b + 1 + NB

        def n_max(v, g):
            return v * G + g + 1

        def n_max_done(v, g):
            return v * G + g + 1 + 2

        def n_small(q, k):
            return q * 3 + k + 4

        def load_stacks(sp, H, s):
            b = H[1]
            ch = slice(s * G * DH, (s + 1) * G * DH)
            for what, dst, row, runs in ((0, q_stack, 0, Q_RUNS), (1, q_stack, REL, Q_RUNS),
                                         (2, k_stack, 0, K_RUNS)):
                for first, count, step in runs:
                    parts = scratch[b, first:first + (count if step else 1), what, ch, :]\
                        .rearrange("i (d g) t -> i d (g t)", g=G)
                    n = count * DH
                    sp.dma_start(dst[row:row + n, s, :, :].rearrange("p g t -> p (g t)"),
                                 parts.broadcast_to((count, DH, G * S))).then_inc(stack_in[s], 16)
                    row += n

        N_STACK = 16 * 3 * len(Q_RUNS)

        def load_shift(sp, q, s, par):
            sp.wait_ge(neg_done, q * 2 + 2)
            for i in range(2):
                sp.dma_start(q_stack[SHIFT + i:SHIFT + i + 1, s, :, :].rearrange("o g (t c) -> o (g t) c", c=P),
                             neg_top[:, par, i, :]).then_inc(shift_in[s], 16)

        def store_split(sp, H):
            if not isinstance(H[0], int) or H[0] > 0:
                for s in range(NQ):
                    sp.wait_ge(stack_in[s], (H[0] - 1) * N_STACK + 16)
            for n in range(NB):
                for what, ready in ((0, 0), (1, 2), (2, 1)):
                    sp.wait_ge(a_pool[n], H[0] * A_POOL + 2 + ready + 1)
                    sp.dma_start(scratch[H[1], :, what, :, n * BLK:(n + 1) * BLK].rearrange("a c t -> c a t"),
                                 split[:, n, :, what, :]).then_inc(split_out, 16)
            sp.wait_ge(split_out, (H[0] + 1) * (16 * 3 * NB) + 16)

        def load_a_weights(sp, l):
            if isinstance(l, int):
                w, v = wa_d[l], va_d[l]
            else:
                w = wa_d[bass.ds(l, 1)].rearrange("o p n -> (o p) n")
                v = va_d[bass.ds(l, 1)].rearrange("o p n -> (o p) n")
            sp.dma_start(wa[:, :, :].rearrange("p a n -> p (a n)"), w).then_inc(wa_in, 16)
            sp.dma_start(va[:, 0:VA - 1], v).then_inc(wa_in, 16)

        def load_d_weights(sp, l):
            if isinstance(l, int):
                w, v, r = wd_d[l], vd_d[l], rows_d[l:l + 1]
            else:
                w = wd_d[bass.ds(l, 1)].rearrange("o p n -> (o p) n")
                v = vd_d[bass.ds(l, 1)].rearrange("o p n -> (o p) n")
                r = rows_d[bass.ds(l, 1)]
            sp.dma_start(wo[:, :], w[:, 0:D]).then_inc(wd_in, 16)
            sp.dma_start(w1[:, :], w[:, D:D + FF]).then_inc(wd_in, 16)
            sp.dma_start(w2[:, :, :].rearrange("p a n -> p (a n)"), w[:, D + FF:D + 2 * FF]).then_inc(wd_in, 16)
            sp.dma_start(vd[:, :], v).then_inc(wd_in, 16)
            sp.dma_start(rows[:, :, :].rearrange("p a n -> p (a n)"), r.broadcast_to((P, 2 * D)))\
              .then_inc(wd_in, 16)

        N_WA, N_WD = 32, 80

        def sp_half(sp, H, b, layer, before=True, more=True):
            nxt = (H + 1, 1 - b)
            if more and b == 1:
                for done, count in ((a_act, A_ACT), (a_dve_n, A_DVE), (a_ready, A_USES)):
                    sp.wait_ge(done, (H + 1) * count)
                    sp.sem_inc(passed, 1)
                load_a_weights(sp, layer + 1)
            load_shift(sp, H * NQ + 1, 1, 1)
            load_shift(sp, H * NQ + 2, 2, 0)
            if more:
                store_split(sp, nxt)
                sp.wait_ge(score_ready, n_score(H * NQ, NU - 1, G - 1))
                load_stacks(sp, nxt, 0)
            load_shift(sp, H * NQ + 3, 3, 1)
            if more:
                sp.wait_ge(score_ready, n_score(H * NQ + 1, NU - 1, G - 1))
                load_stacks(sp, nxt, 1)
                sp.wait_ge(score_ready, n_score(H * NQ + 2, NU - 1, G - 1))
                load_stacks(sp, nxt, 2)
                load_shift(sp, H * NQ + 4, 0, 0)
                sp.wait_ge(score_ready, n_score(H * NQ + 3, NU - 1, G - 1))
                load_stacks(sp, nxt, 3)
            if before and b == 0:
                for done, count in ((d_dve, D_DVE), (d_gelu, NB), (bias_added, 2 * NB)):
                    sp.wait_ge(done, H * count)
                    sp.sem_inc(passed, 1)
                load_d_weights(sp, layer)

        def statistics(dve, chain, base, src, t0, n, eps, stages=(0, 1, 2, 3)):
            for half in range(2):
                if half in stages:
                    for t in range(half * n // 2, (half + 1) * n // 2):
                        nc.vector.bn_stats(stats[:, t, :], src[:, t0 + t, :]).then_inc(chain, 1)
            if 2 in stages:
                dve.wait_ge(chain, base + n)
                dve.sem_inc(passed, 1)
                for t in range(n):
                    nc.vector.bn_aggr(moments[:, t, :], stats[:, t, :]).then_inc(chain, 1)
            if 3 in stages:
                first_root(dve, chain, base, n, eps)
                newton_steps(dve, nc.vector, chain, base, n)

        def first_root(dve, chain, base, n, eps):
            dve.wait_ge(chain, base + 2 * n)
            nc.vector.tensor_scalar(var[:, 0:n], moments[:, 0:n, 1], float(eps), None, ALU.add).then_inc(chain, 1)
            dve.wait_ge(chain, base + 2 * n + 1)
            nc.vector.tensor_scalar(rstd[:, 0:n].bitcast(I32), var[:, 0:n].bitcast(I32), -0.5, float(0x5f3759df),
                                    ALU.mult, ALU.add).then_inc(chain, 1)

        def newton_steps(eng, ops, chain, base, n):
            v, r, w = var[:, 0:n], rstd[:, 0:n], newton[:, 0:n]
            for i in range(NEWTON):
                k = base + 2 * n + 2 + 4 * i
                eng.wait_ge(chain, k)
                ops.tensor_tensor(w, r, r, ALU.mult).then_inc(chain, 1)
                eng.wait_ge(chain, k + 1)
                ops.tensor_tensor(w, w, v, ALU.mult).then_inc(chain, 1)
                eng.wait_ge(chain, k + 2)
                eng.sem_inc(passed, 1)
                ops.tensor_scalar(w, w, -0.5, 1.5, ALU.mult, ALU.add).then_inc(chain, 1)
                eng.wait_ge(chain, k + 3)
                ops.tensor_tensor(r, r, w, ALU.mult).then_inc(chain, 1)

        def centre(dst, src, t, ts):
            return nc.vector.tensor_scalar(dst[:, t, :], src[:, ts, :], moments[:, t, 0:1], rstd[:, t:t + 1],
                                           ALU.subtract, ALU.mult)

        def norm_steps(dve, p, H, b, chain, places, normed):
            stat, aggr, newt, cent = places
            stages = [i for i, at in enumerate((*stat, aggr)) if p == at]
            if stages:
                statistics(dve, chain, H * LN_OPS, h, b * QT, QT, EPS_LAYER, stages)
            if p == newt:
                first_root(dve, chain, H * LN_OPS, QT, EPS_LAYER)
            for n in range(NB):
                if p == cent[n]:
                    if n == 0:
                        dve.wait_ge(chain, (H + 1) * LN_OPS)
                    for t in range(n * TB, (n + 1) * TB):
                        last = centre(centred, h, t, b * QT + t)
                    last.then_inc(normed, 1)

        def a_dve(dve, p, H, b, layer):
            norm_steps(dve, p, H, b, ln_a, (A_STATS, A_AGGR, A_NEWTON, A_CENTRE), a_normed)
            if p == A_NEWTON:
                dve.wait_ge(wa_in, (layer + 1) * N_WA)
                nc.vector.tensor_tensor(va[:, 7:8], va[:, 3:4], va[:, 4:5], ALU.add).then_inc(bias_sum, 1)
                dve.wait_ge(bias_sum, H + 1)
                for n in range(NB):
                    dve.wait_ge(a_pool[n], H * A_POOL + 1)
            for n in range(NB):
                tok = slice(n * BLK, (n + 1) * BLK)
                if p == A_BLOCK[n] + 2:
                    dve.wait_ge(a_act, H * A_ACT + 4 * n + 2)
                    nc.vector.scalar_tensor_tensor(work[:, n, 2, :], work[:, n, 0, :], va[:, 2:3], rot[:, 0, tok],
                                                   ALU.add, ALU.mult).then_inc(a_turned, 1)
                    dve.wait_ge(a_ready, H * A_USES + 5 * n + 3)
                    nc.vector.scalar_tensor_tensor(work[:, n, 3, :], bank_proj[:, :], va[:, 7:8],
                                                   rot[:, 1, tok], ALU.add, ALU.mult).then_inc(a_dve_n, 1)
                for k in range(3):
                    if p != A_BLOCK[n] + A_SUBS[k]:
                        continue
                    if k == 0:
                        dve.wait_ge(a_turned, H * NB + n + 1)
                        dve.wait_ge(a_dve_n, H * A_DVE + n + 1)
                        out, y, op = work[:, n, 2, :], work[:, n, 3, :], ALU.add
                    else:
                        what, src = PARTS[k - 1]
                        dve.wait_ge(a_split[n], H * A_SPLIT + k)
                        out, y, op = work[:, n, src, :], split[:, n, 0, what, :], ALU.subtract
                    nc.vector.tensor_tensor(out, out, y, op).then_inc(a_sub[n], 1)

        def a_pe(pe, p, H, b, layer, first=False):
            for n in range(NB):
                j = p - A_BLOCK[n]
                if not 0 <= j < 5:
                    continue
                if j == 3:
                    pe.wait_ge(a_dve_n, H * A_DVE + n + 1)
                elif j > 0 or n > 0:
                    pe.wait_ge(a_act, H * A_ACT + 4 * n + (0, 1, 2, 0, 3)[j])
                elif not first:
                    pe.wait_ge(d_dve, (H - 1) * D_DVE)
                if j == 0:
                    pe.wait_ge(a_normed, H * NB + n + 1)
                    for t in range(TB):
                        last = nc.tensor.transpose(bank_proj[:, t * P:(t + 1) * P], centred[:, n * TB + t, :],
                                                   ident[:, :])
                elif j < 4:
                    if j == 1 and n == 0:
                        pe.wait_ge(wa_in, (layer + 1) * N_WA)
                    last = nc.tensor.matmul(bank_proj[:, :], wa[:, j - 1, :], xn_t[:, n * BLK:(n + 1) * BLK],
                                            start=True, stop=True)
                else:
                    for t in range(TB):
                        tt = n * TB + t
                        last = nc.tensor.matmul(bank_proj[:, t * P:(t + 1) * P], xn_t[:, tt * P:(tt + 1) * P],
                                                wa[:, 3, :], start=True, stop=True)
                last.then_inc(a_ready, 1)

        PARTS = ((0, 0), (2, 1), (1, 2))

        def a_act_steps(act, p, H, b, layer):
            for n in range(NB):
                j = p - A_BLOCK[n]
                pool = H * A_POOL + 1
                if 0 <= j < 5 and j != 2:
                    if n == 0 and j == 0:
                        act.wait_ge(wa_in, (layer + 1) * N_WA)
                    if j == 0:
                        act.wait_ge(a_pool[n], pool)
                    act.wait_ge(a_ready, H * A_USES + 5 * n + j + 1)
                    if j == 0:
                        nc.scalar.activation(xn_t[:, n * BLK:(n + 1) * BLK], bank_proj[:, :], ACT.Identity,
                                             bias=va[:, 6:7], scale=va[:, 5:6]).then_inc(a_act, 1)
                    elif j == 4:
                        nc.scalar.activation(values[:, b, n * TB:(n + 1) * TB, :, 0:DH],
                                             bank_proj[:, :].rearrange("p (t h d) -> p t h d", t=TB, d=DH),
                                             ACT.Copy).then_inc(a_act, 1)
                    else:
                        i = (j - 1) // 2
                        nc.scalar.activation(work[:, n, i, :], bank_proj[:, :], ACT.Identity, bias=va[:, i:i + 1])\
                          .then_inc(a_act, 1)
                for i, (what, src) in enumerate(PARTS):
                    if j == A_HIGH[i]:
                        if n == 0 and i == 0:
                            act.wait_ge(split_out, H * (16 * 3 * NB) + 16)
                        if what == 1:
                            act.wait_ge(a_sub[n], H * A_SUB + 1)
                        else:
                            act.wait_ge(a_act, H * A_ACT + 4 * n + 2 + i)
                        nc.scalar.activation(split[:, n, 0, what, :], work[:, n, src, :], ACT.Copy)\
                          .then_inc(a_split[n], 1)
                for i, (what, src) in enumerate(PARTS):
                    if j == A_MIDDLE[i]:
                        if i < 2:
                            act.wait_ge(a_sub[n], H * A_SUB + 2 + i)
                        else:
                            act.wait_ge(a_pool[n], pool + 1)
                        nc.scalar.activation(split[:, n, 1, what, :], work[:, n, src, :], ACT.Copy)\
                          .then_inc(a_split[n], 1)

        def a_pool_steps(pool, p, H, b):
            if p == A_NEWTON:
                newton_steps(pool, nc.gpsimd, ln_a, H * LN_OPS, QT)
            for n in range(NB):
                j = p - A_BLOCK[n]
                act_n = H * A_SPLIT
                for k in range(4):
                    if j != A_ADDS[k]:
                        continue
                    low = k > 0
                    what, src = PARTS[k - 1 if low else 2]
                    pool.wait_ge(a_split[n], act_n + 3 + k)
                    x, y, op = work[:, n, src, :], split[:, n, int(low), what, :], ALU.subtract
                    out = split[:, n, 2, what, :] if low else x
                    nc.gpsimd.tensor_tensor(out, x, y, op).then_inc(a_pool[n], 1)

        def d_pe(pe, p, H, b, layer, last_half=False):
            for n in range(NB):
                tok = slice(n * TB, (n + 1) * TB)
                if p == D_CONTEXT[n]:
                    if n == 0:
                        if last_half:
                            pe.wait_ge(d_dve, H * D_DVE)
                        else:
                            pe.wait_ge(a_act, (H + 2) * A_ACT - A_ACT)
                        pe.wait_ge(small_read, n_small(H * NQ + NQ - 1, 2) - last_half)
                        pe.wait_ge(wd_in, (layer + 1) * N_WD)
                    else:
                        pe.wait_ge(d_act, H * D_ACT + n)
                    for t in range(TB):
                        last = nc.tensor.transpose(bank_proj[:, t * P:(t + 1) * P],
                                                   context[:, n * TB + t, :, :].rearrange("p h d -> p (h d)"),
                                                   ident[:, :])
                    last.then_inc(d_ready, 1)
                if p == D_WO[n]:
                    pe.wait_ge(d_act, H * D_ACT + NB)
                    if n:
                        pe.wait_ge(d_dve, H * D_DVE + n)
                    for t in range(TB):
                        tt = n * TB + t
                        last = nc.tensor.matmul(bank_proj[:, t * P:(t + 1) * P], d_t[:, tt * P:(tt + 1) * P],
                                                wo[:, :], start=True, stop=True)
                    last.then_inc(d_ready, 1)
                if p == D_TURN[n]:
                    pe.wait_ge(d_normed, H * NB + n + 1)
                    if n:
                        pe.wait_ge(d_act, H * D_ACT + 3)
                    else:
                        pe.wait_ge(d_dve, H * D_DVE + 2)
                    for t in range(TB):
                        last = nc.tensor.transpose(bank_proj[:, t * P:(t + 1) * P], centred[:, n * TB + t, :],
                                                   ident[:, :])
                    last.then_inc(d_ready, 1)
                f = p - D_UP[n]
                if 0 <= f < FT:
                    pe.wait_ge(d_act, H * D_ACT + 4 + FT * n + f)
                    nc.tensor.matmul(bank_proj[:, :], w1[:, f * P:(f + 1) * P], d_t[:, n * BLK:(n + 1) * BLK],
                                     start=True, stop=True).then_inc(d_ready, 1)
                for t in range(TB):
                    if p != D_DOWN[n][t]:
                        continue
                    if t == 0:
                        pe.wait_ge(d_gelu, H * NB + n + 1)
                        if n:
                            pe.wait_ge(d_dve, H * D_DVE + 3)
                    for f in range(FT):
                        last = nc.tensor.matmul(bank_proj[:, t * P:(t + 1) * P], inner[n][:, f, t * P:(t + 1) * P],
                                                w2[:, f, :], start=f == 0, stop=f == FT - 1)
                    if t == TB - 1:
                        last.then_inc(d_ready, 1)

        def d_act_steps(act, p, H, b, layer):
            for n in range(NB):
                blk = slice(n * BLK, (n + 1) * BLK)
                if p == D_CONTEXT[n]:
                    if n == 0:
                        act.wait_ge(wd_in, (layer + 1) * N_WD)
                    act.wait_ge(d_ready, H * D_USES + n + 1)
                    nc.scalar.activation(d_t[:, blk], bank_proj[:, :], ACT.Identity, bias=vd[:, 0:1])\
                      .then_inc(d_act, 1)
                if p == D_TURN[n]:
                    act.wait_ge(d_ready, H * D_USES + 5 + n)
                    nc.scalar.activation(d_t[:, blk], bank_proj[:, :], ACT.Identity, bias=vd[:, 2:3],
                                         scale=vd[:, 1:2]).then_inc(d_act, 1)
                f = p - D_UP[n]
                if 0 <= f < FT:
                    act.wait_ge(d_ready, H * D_USES + 7 + FT * n + f)
                    nc.scalar.activation(inner[n][:, f, :], bank_proj[:, :], ACT.Identity, bias=vd[:, 3 + f:4 + f])\
                      .then_inc(d_act, 1)
                if p == D_GELU:
                    act.wait_ge(d_act, H * D_ACT + 4 + FT * NB)
                    nc.scalar.activation(inner[n][:, :, :], inner[n][:, :, :], ACT.Gelu).then_inc(d_gelu, 1)

        def d_dve_steps(dve, p, H, b):
            def add_in(n):
                dst = h[:, b * QT + n * TB:b * QT + (n + 1) * TB, :]
                nc.vector.tensor_tensor(dst, dst, bank_proj[:, :].rearrange("p (t c) -> p t c", t=TB), ALU.add)\
                  .then_inc(d_dve, 1)

            for n in range(NB):
                if p == D_WO[n]:
                    dve.wait_ge(bias_added, H * 2 * NB + n + 1)
                    dve.wait_ge(d_ready, H * D_USES + 3 + n)
                    add_in(n)
                if p == D_STATS[n]:
                    dve.wait_ge(d_dve, H * D_DVE + n + 1)
                if p == D_DOWN[n][TB - 1]:
                    dve.wait_ge(bias_added, H * 2 * NB + NB + n + 1)
                    dve.wait_ge(d_ready, H * D_USES + 7 + FT * NB + n)
                    add_in(n)
                if p == A_STATS[n]:
                    dve.wait_ge(d_dve, H * D_DVE + NB + n + 1)
            norm_steps(dve, p, H, b, ln_d, (D_STATS, D_AGGR, D_NEWTON, D_CENTRE), d_normed)

        def d_pool_steps(pool, p, H, b, layer):
            if p == D_NEWTON:
                newton_steps(pool, nc.gpsimd, ln_d, H * LN_OPS, QT)
            for i, places in enumerate((D_ROW, D_ROW2)):
                for n in range(NB):
                    if p == places[n]:
                        if i == 0 and n == 0:
                            pool.wait_ge(wd_in, (layer + 1) * N_WD)
                        if i == 0:
                            pool.wait_ge(a_normed, H * NB + NB)
                        else:
                            pool.wait_ge(d_normed, H * NB + NB)
                        dst = h[:, b * QT + n * TB:b * QT + (n + 1) * TB, :]
                        nc.gpsimd.tensor_tensor(dst, dst, rows[:, i:i + 1, :].broadcast_to((P, TB, D)), ALU.add)\
                          .then_inc(bias_added, 1)

        def slot_of(v_rel):
            quad, c = divmod(v_rel, NU)
            return quad % NQ, quad % 2, c

        def pe_pass1(pe, H, v_rel):
            s, par, c = slot_of(v_rel)
            qt, k0, n = CHUNKS[c]
            v = H * (NQ * NU) + v_rel
            if c == 0:
                pe.wait_ge(stack_in[s], (H + v_rel // NU // NQ + 1) * N_STACK + 16)
            return [(g, qt, k0, n, v, s) for g in range(G)]

        def pe_pass1_one(pe, item):
            g, qt, k0, n, v, s = item
            pe.wait_ge(max_done, n_max_done(v, g) - 2)
            has_diagonal = k0 + n == (qt + 1) * P
            mm = nc.tensor.matmul(bank_max[g % 2][:, 0:n], q_stack[0:SHIFT, s, g, qt * P:(qt + 1) * P],
                                  k_stack[0:SHIFT, s, g, k0:k0 + n], start=True, stop=not has_diagonal)
            if has_diagonal:
                mm = nc.tensor.matmul(bank_max[g % 2][:, n - P:n], ident_b[:, :], mask_b[:, :],
                                      start=False, stop=True)
            mm.then_inc(max_ready, 1)

        def dve_pass1(dve, H, v_rel, midway=None):
            s, par, c = slot_of(v_rel)
            qt, k0, n = CHUNKS[c]
            v = H * (NQ * NU) + v_rel
            dst = top if k0 == 0 else top2
            for g in range(G):
                dve.wait_ge(max_ready, n_max(v, g))
                nc.vector.reduce_max(dst[:, par, g, qt:qt + 1], bank_max[g % 2][:, 0:n], AX.X).then_inc(max_done, 1)
                if g == 1 and midway:
                    midway()
            if c == NU - 1:
                dve.wait_ge(max_done, n_max_done(v, G - 1))
                nc.vector.tensor_tensor(top[:, par, :, TB:QT], top[:, par, :, TB:QT], top2[:, par, :, TB:QT], ALU.max)\
                  .then_inc(merged, 1)

        def pe_top(pe, q, par, small):
            pe.wait_ge(merged, q + 1)
            if small is not None:
                pe.wait_ge(small_read, small - 1)
            nc.tensor.transpose(bank_small[0:G * QT, 0:P], top[:, par, :, :].rearrange("p g t -> p (g t)"),
                                ident[:, :]).then_inc(small_ready, 1)

        def dve_top(dve, q, par, s, small):
            dve.wait_ge(small_ready, small)
            if q is not None:
                dve.wait_ge(neg_done, q * 2)
            dst = neg_top[:, par, :, :]
            nc.vector.tensor_scalar(dst[:, 0, :], bank_small[0:G * QT, 0:P], -1.0, None, ALU.mult).then_inc(neg_done, 1)
            qq = 0 if q is None else q
            dve.wait_ge(neg_done, qq * 2 + 1)
            nc.vector.scalar_tensor_tensor(dst[:, 1, :], bank_small[0:G * QT, 0:P], -1.0, dst[:, 0, :], ALU.mult,
                                           ALU.subtract).then_inc(neg_done, 1)
            dve.wait_ge(neg_done, qq * 2 + 2)
            dve.sem_inc(small_read, 1)

        def pe_scores(pe, H, s, u):
            b, t = UNITS[u]
            first, n = span(u)
            q = H * NQ + s
            if u == 0:
                pe.wait_ge(shift_in[s], (H + 1) * 32 + (16 if s == NQ - 1 else 0))
            return [(q, s, u, g, t, b * BLK + first, n) for g in range(G)]

        def pe_score_one(pe, item):
            q, s, u, g, t, q0, n = item
            pe.wait_ge(exp_done, n_exp(q, u, g) - 2)
            nc.tensor.matmul(bank_score[g % 2][:, 0:n], k_stack[0:ROWS, s, g, t * P:(t + 1) * P],
                             q_stack[0:ROWS, s, g, q0:q0 + n], start=True, stop=True).then_inc(score_ready, 1)

        def act_exps(act, H, s, u, midway):
            first, n = span(u)
            q = H * NQ + s
            act.wait_ge(pv_done, n_pv(q, u) - RING)
            for g in range(G):
                act.wait_ge(score_ready, n_score(q, u, g))
                nc.scalar.activation(probs[:, u % RING, g, 0:n], bank_score[g % 2][:, 0:n], ACT.Exp, scale=SCALE)\
                  .then_inc(exp_done, 1)
                if g == 1:
                    midway()

        def pool_mask(pool, H, s, u):
            q = H * NQ + s
            pool.wait_ge(exp_done, n_exp(q, u, G - 1))
            pool.sem_inc(passed, 1)
            tile = probs[:, u % RING, :, 0:P]
            nc.gpsimd.affine_select(out=tile, in_=tile, compare_op=ALU.is_ge, fill=0.0, base=0,
                                    pattern=[[0, G], [1, P]], channel_multiplier=-1).then_inc(mask_done, 1)

        def pe_pv(pe, q, b, s, u, halves=(0, 1)):
            blk, t = UNITS[u]
            first, n = span(u)
            cut = n // 2 if n > WHOLE else 0
            if 0 in halves and cut or 1 in halves and not cut:
                if diagonal(u):
                    pe.wait_ge(mask_done, n_mask(q, u))
                else:
                    pe.wait_ge(exp_done, n_exp(q, u, G - 1))
                if u == FIRST_OF[blk]:
                    pe.wait_ge(pv_read, n_pv_read(q - 1, blk))
            for i, (lo, hi) in enumerate(((0, cut), (cut, n))):
                if i not in halves or lo == hi:
                    continue
                for g in range(G):
                    last = nc.tensor.matmul(bank_pv[blk][32 * g:32 * g + V_COLS, first + lo:first + hi],
                                            values[:, b, t, s * G + g, :], probs[:, u % RING, g, lo:hi],
                                            start=u == FIRST_OF[blk] and lo == 0,
                                            stop=u == LAST_OF[blk] and hi == n)
                if i == 1:
                    last.then_inc(pv_done, 1)

        def act_pv_out(act, q, blk):
            act.wait_ge(pv_done, n_pv(q, LAST_OF[blk]))
            act.wait_ge(small_ready, n_small(q - 1, 2 * blk))
            nc.scalar.activation(context_raw[:, blk, :], bank_pv[blk][:, :], ACT.Copy).then_inc(pv_read, 1)

        def pe_tail(pe, q, blk, before):
            pe.wait_ge(pv_read, n_pv_read(q, blk))
            pe.wait_ge(small_read, before)
            for t in range(TB):
                last = nc.tensor.transpose(bank_small[:, t * P:(t + 1) * P], context_raw[:, blk, t * P:(t + 1) * P],
                                           ident[:, :])
            last.then_inc(small_ready, 1)

        def dve_tail(dve, q, s, blk, ready):
            dve.wait_ge(small_ready, ready)
            got = bank_small[:, :].rearrange("p (t g c) -> p t g c", t=TB, g=G)
            nc.vector.reciprocal(rden[:, :, :], got[:, :, :, DH]).then_inc(rden_done, 1)
            dve.wait_ge(rden_done, q * NB + blk + 1)
            nc.vector.tensor_tensor(context[:, blk * TB:(blk + 1) * TB, s * G:(s + 1) * G, :], got[:, :, :, 0:DH],
                                    rden[:, :, :].unsqueeze(3).broadcast_to((P, TB, G, DH)), ALU.mult)\
              .then_inc(small_read, 1)

        RAW0, TAIL0, TOP, RAW1, TAIL1 = 6, 8, 9, 2, 3

        def v_exists(more, v_rel):
            return more or v_rel < NQ * NU

        def pe_half(pe, H, b, layers, before=True, more=True):
            def place(p):
                if before:
                    d_pe(pe, p, H - 1, 1 - b, layers[0])
                if more:
                    a_pe(pe, p, H + 1, 1 - b, layers[2])

            for s in range(NQ):
                for u in range(NU):
                    q = H * NQ + s
                    scores = pe_scores(pe, H, s, u)
                    v_rel = s * NU + u + AHEAD
                    maxes = pe_pass1(pe, H, v_rel) if v_exists(more, v_rel) else [None] * G
                    def pv(half):
                        if u >= LAG:
                            pe_pv(pe, q, b, s, u - LAG, half)
                        elif s > 0 or before:
                            pe_pv(pe, q - 1, b if s else 1 - b, (s - 1) % NQ, u - LAG + NU, half)

                    late = before and 2 * (s * NU + u) == D_GELU + 1
                    for g, (a, m) in enumerate(zip(scores, maxes)):
                        if not late or g < 2:
                            pe_score_one(pe, a)
                        if m:
                            pe_pass1_one(pe, m)
                        if g == 1:
                            pv((0,))
                            place(2 * (s * NU + u))
                    pv((1,))
                    if late:
                        place(2 * (s * NU + u) + 1)
                        pe_score_one(pe, scores[2])
                        pe_score_one(pe, scores[3])
                    if u == TAIL0:
                        pe_tail(pe, q, 0, n_small(q, 0) - 1)
                    if u == TOP and (more or s < NQ - 1):
                        pe_top(pe, q + 1, (s + 1) % 2, n_small(q, 1))
                    if u == TAIL1 and (s > 0 or before):
                        pe_tail(pe, q - 1, 1, n_small(q - 1, 2) - 1)
                    if not late:
                        place(2 * (s * NU + u) + 1)

        def act_half(act, H, b, layers, before=True, more=True):
            def place(p):
                if before:
                    d_act_steps(act, p, H - 1, 1 - b, layers[0])
                if more:
                    a_act_steps(act, p, H + 1, 1 - b, layers[2])

            for s in range(NQ):
                for u in range(NU):
                    q = H * NQ + s
                    act_exps(act, H, s, u, lambda: place(2 * (s * NU + u)))
                    if u == RAW0:
                        act_pv_out(act, q, 0)
                    if u == RAW1 and (s > 0 or before):
                        act_pv_out(act, q - 1, 1)
                    place(2 * (s * NU + u) + 1)

        def dve_half(dve, H, b, layers, before=True, more=True):
            def place(p):
                if before:
                    d_dve_steps(dve, p, H - 1, 1 - b)
                if more:
                    a_dve(dve, p, H + 1, 1 - b, layers[2])

            for s in range(NQ):
                for u in range(NU):
                    q = H * NQ + s
                    v_rel = s * NU + u + AHEAD
                    if v_exists(more, v_rel):
                        dve_pass1(dve, H, v_rel, lambda: place(2 * (s * NU + u)))
                    else:
                        place(2 * (s * NU + u))
                    if u == TAIL0:
                        dve_tail(dve, q, s, 0, n_small(q, 0))
                    if u == TOP and (more or s < NQ - 1):
                        dve.wait_ge(shift_in[(s - 1) % NQ], (H + 1) * 32 if s > 0 else H * 32 + 16)
                        dve_top(dve, q + 1, (s + 1) % 2, (s + 1) % NQ, n_small(q, 1))
                    if u == TAIL1 and (s > 0 or before):
                        dve_tail(dve, q - 1, (s - 1) % NQ, 1, n_small(q - 1, 2))
                    place(2 * (s * NU + u) + 1)

        def pool_half(pool, H, b, layers, before=True, more=True):
            def place(p):
                if before:
                    d_pool_steps(pool, p, H - 1, 1 - b, layers[0])
                if more:
                    a_pool_steps(pool, p, H + 1, 1 - b)

            for s in range(NQ):
                for u in range(NU):
                    place(2 * (s * NU + u))
                    if diagonal(u):
                        pool_mask(pool, H, s, u)
                    place(2 * (s * NU + u) + 1)

        def run_halves(eng, half):
            half(eng, 0, 0, (0, 0, 0), before=False)
            with eng.Fori(0, L - 1) as l:
                half(eng, l * 2 + 1, 1, (l, l, l + 1))
                half(eng, l * 2 + 2, 0, (l, l + 1, l + 1))
            half(eng, 2 * L - 1, 1, (L - 1, L - 1, L - 1), more=False)

        LAST = 2 * L - 1
        LAST_Q = 2 * L * NQ - 1

        up_banks = [bank_score[0], bank_score[1], bank_max[0], bank_max[1]]
        down_banks = bank_pv

        INIT = 5
        ROUTER_STEPS = 5 + 3 * E + 3
        N_CONST = 16 * (7 + NQ * G)
        WE = 2 * FF

        up_banks = [bank_score[0], bank_score[1], bank_max[0], bank_max[1]]
        down_banks = bank_pv

        block = ctx.enter_context(nc.Block())

        @block.sync
        def _(sp):
            xv = x_d.rearrange("b (t p) c -> p (b t) c", p=P)
            sp.dma_start(h[:, :, :], xv).then_inc(x_in, 16)
            load_a_weights(sp, 0)
            sp.sem_inc(split_out, 16)
            for s in range(NQ):
                sp.sem_inc(stack_in[s], 16)
            sp.sem_inc(shift_in[NQ - 1], 16)
            for dst, src in ((ident[:, :], ident_d), (ident_b[:, :], identb_d), (mask_b[:, :], maskb_d),
                             (rot[:, :, :], rot_d), (wr[:, :], wr_d), (b2_rows[:, :], be_d[:, 0:D]),
                             (be[:, :, :], be_d[:, D:D + FF].rearrange("e (p f) -> p e f", p=P))):
                sp.dma_start(dst, src).then_inc(const_in, 16)
            for s in range(NQ):
                for g in range(G):
                    sp.dma_start(k_stack[REL:ROWS, s, g, :], kst_d).then_inc(const_in, 16)
            load_d_weights(sp, 0)
            store_split(sp, (0, 0))
            for s in range(NQ):
                load_stacks(sp, (0, 0), s)
            load_shift(sp, 0, 0, 0)

            def half(sp, H, b, layers, before=True, more=True):
                sp_half(sp, H, b, layers[1], before, more)

            run_halves(sp, half)
            sp.wait_ge(d_dve, 2 * L * D_DVE)
            sp.dma_start(probs[:, 0:2, :, :].rearrange("p a g n -> p (a g n)")[:, 0:NT * D]
                         .rearrange("p (t c) -> p t c", c=D), xv).then_inc(x_in, 16)
            for e in range(2):
                sp.dma_start(we[:, e, :], we_d[e]).then_inc(we_in[e], 16)
            with sp.Fori(0, E // 2 - 1) as i:
                for par in range(2):
                    sp.wait_ge(down_ready, (i * 2 + par + 1) * (NB * B) + 2)
                    sp.sem_inc(passed, 1)
                    sp.dma_start(we[:, par, :], we_d[bass.ds(i * 2 + par + 2, 1)].rearrange("o p n -> (o p) n"))\
                      .then_inc(we_in[par], 16)
            sp.wait_ge(down_ready, (E - 1) * (NB * B) + 2)
            sp.dma_start(we[:, 0, :], we_d[E]).then_inc(we_in[0], 16)
            sp.wait_ge(finished, 1)
            sp.dma_start(out_d.rearrange("b (t p) c -> p (b t) c", p=P), acc[:, :, :]).then_inc(out_done, 16)
            sp.wait_ge(out_done, 16)

        @block.gpsimd
        def _(pool):
            for n in range(NB):
                pool.sem_inc(a_pool[n], 1)
            for p in range(PLACES):
                a_pool_steps(pool, p, 0, 0)
            run_halves(pool, pool_half)
            for p in range(PLACES):
                d_pool_steps(pool, p, LAST, 1, L - 1)

        @block.scalar
        def _(act):
            act.sem_inc(exp_done, 2)
            act.sem_inc(pv_read, 2)
            for p in range(PLACES):
                a_act_steps(act, p, 0, 0, 0)
            run_halves(act, act_half)
            act_pv_out(act, LAST_Q, 1)
            for p in range(PLACES):
                d_act_steps(act, p, LAST, 1, L - 1)
            act.sem_inc(gelu_done, 4)
            for n in range(4):
                act.wait_ge(xt_ready, n + 1)
                nc.scalar.activation(x2_t[:, n * 512:(n + 1) * 512], bank_max[n % 2][:, :], ACT.Copy)\
                  .then_inc(xt_read, 1)
            act.wait_ge(router, 2)
            nc.scalar.activation(prob_e[:, :, :], logit[:, :, :], ACT.Exp).then_inc(router_exp, 1)
            for n in range(4):
                act.wait_ge(gates_ready, n + 1)
                nc.scalar.activation(gates_t[:, n * 512:(n + 1) * 512], bank_max[n % 2][0:EXPERTS, :], ACT.Copy)\
                  .then_inc(gates_read, 1)
            for n in range(4):
                act.wait_ge(b2_ready, n + 1)
                nc.scalar.activation(acc[:, n * TB:(n + 1) * TB, :],
                                     bank_max[n % 2][:, :].rearrange("p (t c) -> p t c", t=TB), ACT.Copy)\
                  .then_inc(b2_read, 1)

            def expert(e, par, col):
                for n in range(NB * B):
                    act.wait_ge(down_ready, e * 4 + n + 1)
                    for f in range(FT):
                        act.wait_ge(up_ready, e * 16 + 4 * n + f + 1)
                        nc.scalar.activation(probs[:, 2 + n % 2, f, :], up_banks[f][:, :], ACT.Gelu_apprx_tanh,
                                             bias=b1_now[:, par, f:f + 1]).then_inc(gelu_done, 1)

            with act.Fori(0, E // 2) as i:
                for par in range(2):
                    act.wait_ge(gate_copied, i * 2 + par + 1)
                    expert(i * 2 + par, par, None)
            act.wait_ge(gate_copied, E + 1)
            expert(E, 0, None)

        @block.tensor
        def _(pe):
            pe.sem_inc(pv_done, RING)
            pe.sem_inc(small_ready, 2)
            pe.wait_ge(const_in, N_CONST)
            pe.wait_ge(init_done, INIT)
            for p in range(PLACES):
                a_pe(pe, p, 0, 0, 0, first=True)
            for v in range(AHEAD):
                for item in pe_pass1(pe, 0, v):
                    pe_pass1_one(pe, item)
                if v == NU - 1:
                    pe_top(pe, 0, 0, None)
            run_halves(pe, pe_half)
            for u in range(NU - LAG, NU):
                pe_pv(pe, LAST_Q, 1, NQ - 1, u)
            pe_tail(pe, LAST_Q, 1, n_small(LAST_Q, 2) - 2)
            for p in range(PLACES):
                d_pe(pe, p, LAST, 1, L - 1, last_half=True)
            pe.sem_inc(down_ready, 2)
            for n in range(4):
                pe.wait_ge(x_normed, n + 1)
                if n >= 2:
                    pe.wait_ge(xt_read, n - 1)
                for t in range(TB):
                    last = nc.tensor.transpose(bank_max[n % 2][:, t * P:(t + 1) * P], acc[:, n * TB + t, :],
                                               ident[:, :])
                last.then_inc(xt_ready, 1)
            pe.wait_ge(xt_read, 4)
            for t in range(NT):
                last = nc.tensor.matmul(bank_proj[:, t * E:(t + 1) * E], x2_t[:, t * P:(t + 1) * P], wr[:, :],
                                        start=True, stop=True)
            last.then_inc(router_done, 1)
            pe.wait_ge(router, ROUTER_STEPS)
            for n in range(4):
                if n >= 2:
                    pe.wait_ge(gates_read, n - 1)
                for t in range(TB):
                    last = nc.tensor.transpose(bank_max[n % 2][0:EXPERTS, t * P:(t + 1) * P],
                                               gates[:, n * TB + t, :], ident[:, :])
                last.then_inc(gates_ready, 1)
            pe.wait_ge(gates_read, 4)
            for n in range(4):
                if n >= 2:
                    pe.wait_ge(b2_read, n - 1)
                for t in range(TB):
                    tt = n * TB + t
                    last = nc.tensor.matmul(bank_max[n % 2][:, t * P:(t + 1) * P], gates_t[:, tt * P:(tt + 1) * P],
                                            b2_rows[:, :], start=True, stop=True)
                last.then_inc(b2_ready, 1)
            pe.wait_ge(b2_read, 4)

            def up(e, par, n):
                for f in range(FT):
                    pe.wait_ge(gelu_done, e * 16 + 4 * n + f + 1)
                    nc.tensor.matmul(up_banks[f][:, :], we[:, par, f * P:(f + 1) * P],
                                     x2_t[:, n * 512:(n + 1) * 512], start=True, stop=True).then_inc(up_ready, 1)

            def down(e, par, n):
                pe.wait_ge(gelu_done, e * 16 + 4 * n + FT + 4)
                pe.wait_ge(acc_done, e * 4 + n + 1)
                for t in range(TB):
                    for f in range(FT):
                        last = nc.tensor.matmul(down_banks[n % 2][:, t * P:(t + 1) * P],
                                                probs[:, 2 + n % 2, f, t * P:(t + 1) * P],
                                                we[:, par, FF + f * D:FF + (f + 1) * D],
                                                start=f == 0, stop=f == FT - 1)
                last.then_inc(down_ready, 1)

            def expert(e, par, arrived):
                pe.wait_ge(we_in[par], arrived)
                up(e, par, 0)
                for n in range(1, NB * B):
                    up(e, par, n)
                    down(e, par, n - 1)
                down(e, par, NB * B - 1)

            with pe.Fori(0, E // 2) as i:
                for par in range(2):
                    expert(i * 2 + par, par, i * 16 + 16)
            expert(E, 0, 16 * (E // 2 + 1))

        @block.vector
        def _(dve):
            nc.vector.memset(values[:, :, :, :, DH:V_COLS], 1.0).then_inc(init_done, 1)
            for b in bank_pv:
                nc.vector.memset(b[:, :], 0.0).then_inc(init_done, 1)
            nc.vector.memset(gates[:, :, E:E + 1], 1.0).then_inc(init_done, 1)
            nc.vector.memset(gates_e[:, E, :], 1.0).then_inc(init_done, 1)
            dve.sem_inc(max_done, 2)
            dve.sem_inc(small_read, 2)
            dve.wait_ge(x_in, 16)
            statistics(dve, ln_x, 0, h, 0, NT, EPS_OUT)
            n_x = LN_OPS + 2 * QT
            dve.wait_ge(ln_x, n_x)
            for t in range(NT):
                centre(h, h, t, t).then_inc(ln_x, 1)
            dve.wait_ge(ln_x, n_x + NT)
            dve.wait_ge(const_in, N_CONST)
            for p in range(PLACES):
                a_dve(dve, p, 0, 0, 0)
            for v in range(AHEAD):
                dve_pass1(dve, 0, v)
                if v == NU - 1:
                    dve_top(dve, None, 0, 0, 3)
            run_halves(dve, dve_half)
            dve_tail(dve, LAST_Q, NQ - 1, 1, n_small(LAST_Q, 2) - 1)
            for p in range(PLACES):
                d_dve_steps(dve, p, LAST, 1)
            dve.wait_ge(x_in, 32)
            x_again = probs[:, 0:2, :, :].rearrange("p a g n -> p (a g n)")[:, 0:NT * D]\
                .rearrange("p (t c) -> p t c", c=D)
            nc.vector.tensor_tensor(h[:, :, :], h[:, :, :], x_again, ALU.add).then_inc(ln_x, 1)
            n_x += NT + 1
            dve.wait_ge(ln_x, n_x)
            statistics(dve, ln_x, n_x, h, 0, NT, EPS_OUT)
            dve.wait_ge(ln_x, n_x + LN_OPS + 2 * QT)
            for t in range(NT):
                last = centre(acc, h, t, t)
                if t % TB == TB - 1:
                    last.then_inc(x_normed, 1)
            count = [0]

            def step(ins):
                ins.then_inc(router, 1)
                count[0] += 1
                dve.wait_ge(router, count[0])

            dve.wait_ge(router_done, 1)
            got = bank_proj[:, 0:NT * E].rearrange("p (t e) -> p t e", e=E)
            step(nc.vector.tensor_reduce(one_col[:, :], got, AX.X, ALU.max))
            step(nc.vector.tensor_tensor(logit[:, :, :], got, one_col[:, :].unsqueeze(2).broadcast_to((P, NT, E)),
                                         ALU.subtract))
            dve.wait_ge(router_exp, 1)
            step(nc.vector.tensor_reduce(one_col[:, :], prob_e[:, :, :], AX.X, ALU.add))
            step(nc.vector.reciprocal(one_col[:, :], one_col[:, :]))
            step(nc.vector.tensor_tensor(prob_e[:, :, :], prob_e[:, :, :],
                                         one_col[:, :].unsqueeze(2).broadcast_to((P, NT, E)), ALU.mult))
            for o in range(E):
                other = prob_e[:, :, o:o + 1]
                last = None
                if o > 0:
                    last = nc.vector.tensor_tensor(cmp[:, :, 0:o], other.broadcast_to((P, NT, o)),
                                                   prob_e[:, :, 0:o], ALU.is_gt)
                if last is not None:
                    step(last)
                else:
                    step(nc.vector.memset(rank[:, :, :], 0.0))
                step(nc.vector.tensor_tensor(cmp[:, :, o:E], other.broadcast_to((P, NT, E - o)), prob_e[:, :, o:E],
                                             ALU.is_ge))
                step(nc.vector.tensor_tensor(rank[:, :, :], rank[:, :, :], cmp[:, :, :], ALU.add))
            step(nc.vector.tensor_scalar(cmp[:, :, :], rank[:, :, :], 2.5, None, ALU.is_lt))
            step(nc.vector.tensor_tensor(gates[:, :, 0:E], cmp[:, :, :], prob_e[:, :, :], ALU.mult))
            step(nc.vector.tensor_copy(gates_e[:, 0:E, :], gates[:, :, 0:E].rearrange("p t e -> p e t")))
            assert count[0] == ROUTER_STEPS
            dve.sem_inc(acc_done, 2)
            dve.wait_ge(b2_read, 4)

            def expert(e, par):
                for n in range(NB * B):
                    dve.wait_ge(down_ready, e * 4 + n + 3)
                    for t in range(TB):
                        tt = n * TB + t
                        last = nc.vector.scalar_tensor_tensor(acc[:, tt, :], down_banks[n % 2][:, t * P:(t + 1) * P],
                                                              gate_now[:, par, tt:tt + 1], acc[:, tt, :], ALU.mult,
                                                              ALU.add)
                    last.then_inc(acc_done, 1)

            def take_gates(e, par, at):
                nc.vector.tensor_copy(b1_now[:, par, :].unsqueeze(1), be[:, at, :])
                nc.vector.tensor_copy(gate_now[:, par, :].unsqueeze(1), gates_e[:, at, :]).then_inc(gate_copied, 1)
                dve.wait_ge(gate_copied, e + 1)

            with dve.Fori(0, E // 2) as i:
                for par in range(2):
                    e = i * 2 + par
                    take_gates(e, par, bass.ds(e, 1))
                    expert(e, par)
            take_gates(E, 0, slice(E, E + 1))
            expert(E, 0)
            dve.wait_ge(acc_done, EXPERTS * 4 + 2)
            nc.vector.scalar_tensor_tensor(acc[:, :, :], acc[:, :, :], MOE_SCALE, h[:, :, :], ALU.mult, ALU.add)\
              .then_inc(finished, 1)


def bf16_bits(a):
    b = np.ascontiguousarray(a, np.float32).view(np.uint32)
    return ((b + np.uint32(0x7fff) + ((b >> 16) & np.uint32(1))) >> 16).astype(np.uint16)


def rounded(a):
    return (bf16_bits(a).astype(np.uint32) << 16).view(np.float32)


def constants():
    half = DH // 2
    inv = (1.0 / np.float32(10000.0) ** (np.arange(0, DH, 2, dtype=np.float32) / DH)).astype(np.float32)
    angle = np.arange(S, dtype=np.float64)[None, :] * inv.astype(np.float64)[:, None]
    sin, cos = np.sin(angle), np.cos(angle)
    ch = ORDER % DH
    f = ch % half
    rot = np.stack([sin[f], np.where((ch < half)[:, None], cos[f], -cos[f])], axis=1).astype(np.float32)
    table = np.concatenate([cos, sin], axis=0).astype(np.float32)
    high = rounded(table)
    middle = rounded(table - high)
    low = rounded(table - high - middle)
    parts = (high, middle, low)
    kst = np.concatenate([parts[i] for i in K_PARTS] + [np.ones((2, S), np.float32)], axis=0)
    ident = np.eye(P, dtype=np.float32)
    mask = np.where(np.arange(P)[None, :] > np.arange(P)[:, None], np.float32(NEG), np.float32(0))
    return ident, bf16_bits(ident), bf16_bits(mask), rot, bf16_bits(kst)


def kernel(**inp):
    import concourse.bacc as bacc
    from concourse.bass_utils import run_bass_kernel_spmd
    a = {k: np.asarray(v) for k, v in inp.items()}
    A = {k[8:]: v for k, v in a.items() if k.startswith("L0_attn_")}
    M = {k[7:]: v for k, v in a.items() if k.startswith("L0_ffn_")}
    swap = ORDER.reshape(NQ, 2, DH // 2, G)[:, ::-1].reshape(P)
    t = lambda w: np.swapaxes(w, -1, -2)
    u = A["u_bias"].reshape(L, D)
    wa = np.concatenate([t(A["Wq"][:, ORDER]), t(A["Wq"][:, swap]), t(A["Wk"][:, ORDER]), t(A["Wv"])], axis=2)
    va = np.stack([A["bq"][:, ORDER], A["bk"][:, ORDER], u[:, ORDER], A["bq"][:, swap], u[:, swap], A["ln1_w"],
                   A["ln1_b"]], axis=2)
    tiles = lambda w: np.swapaxes(t(w).reshape(w.shape[0], FT, P, D), 1, 2).reshape(w.shape[0], P, FT * D)
    wd = np.concatenate([t(A["Wo"]), t(A["W1"]), tiles(A["W2"])], axis=2)
    vd = np.concatenate([np.stack([A["bv"], A["ln2_w"], A["ln2_b"]], axis=2),
                         np.swapaxes(A["b1"].reshape(L, FT, P), 1, 2), A["bv"][:, :, None]], axis=2)
    rows = np.concatenate([A["bo"], A["b2"]], axis=1)
    w1 = np.concatenate([t(M["W1"]), t(M["Ws1"])[None]], axis=0)
    w2 = np.concatenate([tiles(M["W2"]), tiles(M["Ws2"][None])], axis=0)
    we = np.concatenate([w1, w2], axis=2)
    b1 = np.concatenate([M["b1"], M["bs1"][None]], axis=0).reshape(EXPERTS, FT, P)
    b2 = np.concatenate([M["b2"], M["bs2"][None]], axis=0)
    be = np.concatenate([b2, np.swapaxes(b1, 1, 2).reshape(EXPERTS, FF)], axis=1)
    given = {"x": A["x"], "wa": wa, "va": va, "wd": wd, "vd": vd, "rows": rows, "wr": t(M["w_router"]), "we": we,
             "be": be}
    given |= dict(zip(("ident", "ident_b", "mask_b", "rot", "kst"), constants()))
    nc = bacc.Bacc("TRN2", target_bir_lowering=False, num_devices=1)
    arrays, args = {}, []
    for name, v in given.items():
        v = np.ascontiguousarray(v)
        arrays[f"in_{name}"] = v
        ap = nc.dram_tensor(f"in_{name}", v.shape, mybir.dt.from_np(v.dtype), kind="ExternalInput").ap()
        args.append(ap.bitcast(BF16) if v.dtype == np.uint16 else ap)
    args.append(nc.dram_tensor("out", (B, S, D), F32, kind="ExternalOutput").ap())
    build(nc, *args)
    r = run_bass_kernel_spmd(nc, [arrays], core_ids=[0])
    return r.results[0]["out"]
```

```python
import concourse.bass as bass
from concourse import mybir
from contextlib import ExitStack
import numpy as np

F32 = mybir.dt.float32
BF16 = mybir.dt.bfloat16
I32 = mybir.dt.int32
ALU = mybir.AluOpType
ACT = mybir.ActivationFunctionType
AX = mybir.AxisListType

B, S, D = 2, 1024, 128
L, NH, DH = 4, 16, 8
FF, E = 512, 8
P = 128
QT = S // P
BLK = 512
NB = S // BLK
TB = BLK // P
G = 4
NQ = NH // G
FT = FF // P
NT = B * QT
EXPERTS = E + 1
SCALE = float(DH) ** -0.5
MOE_SCALE = 1.0 / float(np.sqrt(1 + 2 / E))
NEG = -3.0e38
EPS_OUT, EPS_LAYER = 1e-5, 1e-6

Q_PARTS = (0, 0, 0, 1, 1, 2)
K_PARTS = (0, 1, 2, 0, 1, 0)
Q_RUNS = ((0, 3, 0), (1, 2, 0), (2, 1, 0))
K_RUNS = ((0, 3, 1), (0, 2, 1), (0, 1, 1))
NP = len(Q_PARTS)
REL = NP * DH
SHIFT = 2 * REL
ROWS = SHIFT + 2

UNITS = [(0, 0), (0, 3), (0, 1), (0, 2), (1, 0), (1, 5), (1, 1), (1, 7), (1, 2), (1, 6), (1, 3), (1, 4)]
CHUNKS = [(1, 0, 256), (3, 0, 512), (4, 0, 512), (5, 0, 512), (0, 0, 128), (2, 0, 384), (5, 512, 256),
          (6, 0, 512), (6, 512, 384), (7, 0, 512), (4, 512, 128), (7, 512, 512)]
NU = len(UNITS)
AHEAD = NU + 3
FIRST_OF = [0, 4]
LAST_OF = [3, NU - 1]
WHOLE = 256
LAG = 2
RING = 4

V_COLS = DH + 1
A_USES, A_ACT, A_DVE = 10, 8, 2
A_POOL, A_SPLIT, A_PARTS, A_SUB = 4, 3, 3, 3
D_USES, D_ACT, D_DVE = 16, 12, 4
NEWTON = 3
LN_OPS = 2 * QT + 2 + 4 * NEWTON
VA, VD = 8, 8

D_ROW = (4, 6)
D_CONTEXT, D_WO = (8, 9), (10, 11)
D_STATS, D_AGGR, D_NEWTON, D_CENTRE = (11, 13), 14, 15, ((18, 18), (19, 19))
D_ROW2 = (19, 20)
D_TURN = (19, 20)
D_UP, D_GELU = (21, 25), 29
D_DOWN = ((31, 31, 31, 31), (32, 33, 34, 35))
A_STATS, A_AGGR, A_NEWTON, A_CENTRE = (33, 36), 38, 39, ((42, 43), (44, 45))
A_BLOCK = (44, 49)
A_HIGH, A_MIDDLE, A_COPIES = (2, 4), 4, (3, 5, 6)
A_SUBS = (3, 3, 5)
A_ADDS = (5, 5, 7, 7)
PLACES = A_BLOCK[1] + A_ADDS[-1] + 1

F_ADD, F_STATS, F_AGGR, F_ROOT, F_CENTRE = 40, (42, 43), 44, 45, 46
F_TURN, F_ROUTER, F_CHAIN = (50, 51), 52, 53
ROUTER_STEPS = 5 + 3 * E + 3
F_GATES = (F_CHAIN + ROUTER_STEPS, F_CHAIN + ROUTER_STEPS + 1)
F_B2 = (F_GATES[1] + 1, F_GATES[1] + 2)
F_PLACES = F_B2[1] + 1
UP_AT, GELU_AT, DOWN_AT, ACC_AT = (0, 5, 12, 28), (0, 5, 12, 30), (7, 14, 30, 36), (9, 20, 32)

ORDER = np.arange(P).reshape(NQ, G, DH).transpose(0, 2, 1).reshape(P)


def diagonal(u):
    b, t = UNITS[u]
    return t >= TB * b


def span(u):
    b, t = UNITS[u]
    first = max(0, t - TB * b) * P
    return first, BLK - first


MASKED = [u for u in range(NU) if diagonal(u)]


def build(nc, x_d, wa_d, va_d, wd_d, vd_d, rows_d, wr_d, we_d, be_d, ident_d, identb_d, maskb_d, rot_d, kst_d,
          out_d):
    ctx = ExitStack()
    with ctx:
        def sb(name, shape, dt=F32):
            return ctx.enter_context(nc.sbuf_tensor(name, shape, dt))

        def sem(name):
            return ctx.enter_context(nc.semaphore(name))

        scratch = nc.dram_tensor("split_scratch", [B, 3, 3, D, S], BF16, kind="Internal").ap()

        q_stack = sb("q_stack", [P, NQ, G, S], BF16)
        k_stack = sb("k_stack", [P, NQ, G, S], BF16)
        probs = sb("probs", [P, RING, G, BLK])
        values = sb("values", [P, B, QT, NH, V_COLS])
        h = sb("h", [P, NT, D])
        xn_t = sb("xn_t", [P, S])
        d_t = sb("d_t", [P, S])
        centred = sb("centred", [P, QT, D])
        rot = sb("rot", [P, 2, S])
        split = sb("split", [P, NB, 3, 3, BLK], BF16)
        work = sb("work", [P, NB, 4, BLK])
        wa = sb("wa", [P, 4, D])
        va = sb("va", [P, VA])
        wo = sb("wo", [P, D])
        w1 = sb("w1", [P, FF])
        w2 = sb("w2", [P, FT, D])
        vd = sb("vd", [P, VD])
        rows = sb("rows", [P, 2, D])
        context_raw = sb("context_raw", [P, NB, BLK])
        context = sb("context", [P, QT, NH, DH])
        rden = sb("rden", [P, TB, G])
        top = sb("top", [P, 2, G, QT])
        top2 = sb("top2", [P, 2, G, QT])
        neg_top = sb("neg_top", [G * QT, 2, 2, P], BF16)
        stats = sb("stats", [P, NT, 6])
        moments = sb("moments", [P, NT, 2])
        var = sb("var", [P, NT])
        rstd = sb("rstd", [P, NT])
        newton = sb("newton", [P, NT])
        ident = sb("ident", [P, P])
        ident_b = sb("ident_b", [P, P], BF16)
        mask_b = sb("mask_b", [P, P], BF16)
        acc = sb("acc", [P, NT, D])
        we = sb("we", [P, 2, 2 * FF])
        inner = [acc[:, :, :].rearrange("p a b -> p (a b)").rearrange("p (f n) -> p f n", f=FT),
                 we[:, :, :].rearrange("p a b -> p (a b)").rearrange("p (f n) -> p f n", f=FT)]
        k_flat = k_stack[:, :, :, :].rearrange("p s g t -> p (s g t)").bitcast(F32)
        inner_last = [k_flat[:, n * FT * BLK:(n + 1) * FT * BLK].rearrange("p (f n) -> p f n", f=FT)
                      for n in range(NB)]
        x_again = q_stack[:, 0, :, :].rearrange("p g t -> p (g t)").bitcast(F32)\
            .rearrange("p (t c) -> p t c", c=D)
        be = sb("be", [P, EXPERTS, FT])
        b1_now = sb("b1_now", [P, 2, FT])
        gate_now = sb("gate_now", [P, 2, NT])
        wr = sb("wr", [P, E])
        b2_rows = sb("b2_rows", [EXPERTS, D])
        logit = sb("logit", [P, NT, E])
        prob_e = sb("prob_e", [P, NT, E])
        rank = sb("rank", [P, NT, E])
        cmp = sb("cmp", [P, NT, E])
        one_col = sb("one_col", [P, NT])
        gates = sb("gates", [P, NT, EXPERTS])
        gates_e = sb("gates_e", [P, EXPERTS, NT])
        flat = work[:, :, :, :].rearrange("p a b c -> p (a b c)")
        x2_t = flat[:, 0:NT * P]
        gates_t = flat[0:EXPERTS, NT * P:2 * NT * P]

        def bank(name):
            return ctx.enter_context(nc.psum_tensor(name, [P, 512], F32))

        bank_max = [bank("bank_max0"), bank("bank_max1")]
        bank_score = [bank("bank_score0"), bank("bank_score1")]
        bank_pv = [bank("bank_pv0"), bank("bank_pv1")]
        bank_small = bank("bank_small")
        bank_proj = bank("bank_proj")

        const_in = sem("const_in")
        x_in = [sem(f"x_in{b}") for b in range(B)]
        x_again_in = sem("x_again_in")
        wa_in, wd_in = sem("wa_in"), sem("wd_in")
        stack_in = [sem(f"stack_in{s}") for s in range(NQ)]
        shift_in = [sem(f"shift_in{s}") for s in range(NQ)]
        split_out = sem("split_out")
        init_done = sem("init_done")
        passed = sem("passed")
        score_ready = sem("score_ready")
        exp_done = sem("exp_done")
        mask_done = sem("mask_done")
        pv_done = sem("pv_done")
        pv_read = sem("pv_read")
        max_ready = sem("max_ready")
        max_done = sem("max_done")
        merged = sem("merged")
        small_ready = sem("small_ready")
        small_read = sem("small_read")
        neg_done = sem("neg_done")
        rden_done = sem("rden_done")
        bias_sum = sem("bias_sum")
        a_ready, a_act, a_second = sem("a_ready"), sem("a_act"), sem("a_second")
        a_turned = sem("a_turned")
        a_split = [sem(f"a_split{n}") for n in range(NB)]
        a_parts = [sem(f"a_parts{n}") for n in range(NB)]
        a_sub = [sem(f"a_sub{n}") for n in range(NB)]
        a_pool = [sem(f"a_pool{n}") for n in range(NB)]
        a_normed, d_normed = sem("a_normed"), sem("d_normed")
        d_ready, d_act, d_dve = sem("d_ready"), sem("d_act"), sem("d_dve")
        d_gelu = sem("d_gelu")
        bias_added = sem("bias_added")
        ln_a, ln_d, ln_x = sem("ln_a"), sem("ln_d"), sem("ln_x")
        x_normed = sem("x_normed")
        xt_ready, xt_read = sem("xt_ready"), sem("xt_read")
        router_done, router = sem("router_done"), sem("router")
        router_exp = sem("router_exp")
        gates_ready, gates_read = sem("gates_ready"), sem("gates_read")
        b2_ready, b2_read = sem("b2_ready"), sem("b2_read")
        we_in = [sem("we_in0"), sem("we_in1")]
        up_ready, gelu_done = sem("up_ready"), sem("gelu_done")
        down_ready, acc_done = sem("down_ready"), sem("acc_done")
        gate_copied, gates_late = sem("gate_copied"), sem("gates_late")
        finished, out_done = sem("finished"), sem("out_done")

        def n_score(q, u, g):
            return (q * NU + u) * G + g + 1

        def n_exp(q, u, g):
            return (q * NU + u) * G + g + 1 + 2

        def n_mask(q, u):
            return q * len(MASKED) + MASKED.index(u) + 1

        def n_pv(q, u):
            return q * NU + u + 1 + RING

        def n_pv_read(q, b):
            return q * NB + b + 1 + NB

        def n_max(v, g):
            return v * G + g + 1

        def n_max_done(v, g):
            return v * G + g + 1 + 2

        def n_small(q, k):
            return q * 3 + k + 4

        xv = x_d.rearrange("b (t p) c -> p (b t) c", p=P)

        def load_stacks(sp, H, s):
            b = H[1]
            ch = slice(s * G * DH, (s + 1) * G * DH)
            for what, dst, row, runs in ((0, q_stack, 0, Q_RUNS), (1, q_stack, REL, Q_RUNS),
                                         (2, k_stack, 0, K_RUNS)):
                for first, count, step in runs:
                    parts = scratch[b, first:first + (count if step else 1), what, ch, :]\
                        .rearrange("i (d g) t -> i d (g t)", g=G)
                    n = count * DH
                    sp.dma_start(dst[row:row + n, s, :, :].rearrange("p g t -> p (g t)"),
                                 parts.broadcast_to((count, DH, G * S))).then_inc(stack_in[s], 16)
                    row += n

        N_STACK = 16 * 3 * len(Q_RUNS)

        def load_shift(sp, q, s, par):
            sp.wait_ge(neg_done, q * 2 + 2)
            for i in range(2):
                sp.dma_start(q_stack[SHIFT + i:SHIFT + i + 1, s, :, :].rearrange("o g (t c) -> o (g t) c", c=P),
                             neg_top[:, par, i, :]).then_inc(shift_in[s], 16)

        def store_split(sp, H):
            if not isinstance(H[0], int) or H[0] > 0:
                for s in range(NQ):
                    sp.wait_ge(stack_in[s], (H[0] - 1) * N_STACK + 16)
            for n in range(NB):
                for what, ready in ((0, 0), (1, 2), (2, 1)):
                    sp.wait_ge(a_pool[n], H[0] * A_POOL + 2 + ready + 1)
                    sp.dma_start(scratch[H[1], :, what, :, n * BLK:(n + 1) * BLK].rearrange("a c t -> c a t"),
                                 split[:, n, :, what, :]).then_inc(split_out, 16)
            sp.wait_ge(split_out, (H[0] + 1) * (16 * 3 * NB) + 16)

        def load_a_weights(sp, l):
            if isinstance(l, int):
                w, v = wa_d[l], va_d[l]
            else:
                w = wa_d[bass.ds(l, 1)].rearrange("o p n -> (o p) n")
                v = va_d[bass.ds(l, 1)].rearrange("o p n -> (o p) n")
            sp.dma_start(wa[:, :, :].rearrange("p a n -> p (a n)"), w).then_inc(wa_in, 16)
            sp.dma_start(va[:, 0:VA - 1], v).then_inc(wa_in, 16)

        def load_d_weights(sp, l):
            if isinstance(l, int):
                w, v, r = wd_d[l], vd_d[l], rows_d[l:l + 1]
            else:
                w = wd_d[bass.ds(l, 1)].rearrange("o p n -> (o p) n")
                v = vd_d[bass.ds(l, 1)].rearrange("o p n -> (o p) n")
                r = rows_d[bass.ds(l, 1)]
            sp.dma_start(wo[:, :], w[:, 0:D]).then_inc(wd_in, 16)
            sp.dma_start(w1[:, :], w[:, D:D + FF]).then_inc(wd_in, 16)
            sp.dma_start(w2[:, :, :].rearrange("p a n -> p (a n)"), w[:, D + FF:D + 2 * FF]).then_inc(wd_in, 16)
            sp.dma_start(vd[:, :], v).then_inc(wd_in, 16)
            sp.dma_start(rows[:, :, :].rearrange("p a n -> p (a n)"), r.broadcast_to((P, 2 * D)))\
              .then_inc(wd_in, 16)

        N_WA, N_WD = 32, 80

        def sp_half(sp, H, b, layer, before=True, more=True):
            nxt = (H + 1, 1 - b)
            if more and b == 1:
                for done, count in ((a_act, A_ACT), (a_second, A_DVE), (a_ready, A_USES)):
                    sp.wait_ge(done, (H + 1) * count)
                    sp.sem_inc(passed, 1)
                load_a_weights(sp, layer + 1)
            load_shift(sp, H * NQ + 1, 1, 1)
            if not more:
                sp.wait_ge(score_ready, n_score(H * NQ, NU - 1, G - 1))
                sp.dma_start(x_again, xv).then_inc(x_again_in, 16)
            load_shift(sp, H * NQ + 2, 2, 0)
            if not more:
                sp.wait_ge(d_dve, H * D_DVE)
                for e in range(2):
                    sp.dma_start(we[:, e, :], we_d[e]).then_inc(we_in[e], 16)
            if more:
                store_split(sp, nxt)
                sp.wait_ge(score_ready, n_score(H * NQ, NU - 1, G - 1))
                load_stacks(sp, nxt, 0)
            load_shift(sp, H * NQ + 3, 3, 1)
            if more:
                sp.wait_ge(score_ready, n_score(H * NQ + 1, NU - 1, G - 1))
                load_stacks(sp, nxt, 1)
                sp.wait_ge(score_ready, n_score(H * NQ + 2, NU - 1, G - 1))
                load_stacks(sp, nxt, 2)
                load_shift(sp, H * NQ + 4, 0, 0)
                sp.wait_ge(score_ready, n_score(H * NQ + 3, NU - 1, G - 1))
                load_stacks(sp, nxt, 3)
            if before and b == 0:
                for done, count in ((d_dve, D_DVE), (d_gelu, NB), (bias_added, 2 * NB)):
                    sp.wait_ge(done, H * count)
                    sp.sem_inc(passed, 1)
                load_d_weights(sp, layer)

        def statistics(dve, chain, base, src, t0, n, eps, stages=(0, 1, 2, 3)):
            for half in range(2):
                if half in stages:
                    for t in range(half * n // 2, (half + 1) * n // 2):
                        nc.vector.bn_stats(stats[:, t, :], src[:, t0 + t, :]).then_inc(chain, 1)
            if 2 in stages:
                dve.wait_ge(chain, base + n)
                dve.sem_inc(passed, 1)
                for t in range(n):
                    nc.vector.bn_aggr(moments[:, t, :], stats[:, t, :]).then_inc(chain, 1)
            if 3 in stages:
                first_root(dve, chain, base, n, eps)
                newton_steps(dve, nc.vector, chain, base, n)

        def first_root(dve, chain, base, n, eps):
            dve.wait_ge(chain, base + 2 * n)
            nc.vector.tensor_scalar(var[:, 0:n], moments[:, 0:n, 1], float(eps), None, ALU.add).then_inc(chain, 1)
            dve.wait_ge(chain, base + 2 * n + 1)
            nc.vector.tensor_scalar(rstd[:, 0:n].bitcast(I32), var[:, 0:n].bitcast(I32), -0.5, float(0x5f3759df),
                                    ALU.mult, ALU.add).then_inc(chain, 1)

        def newton_steps(eng, ops, chain, base, n):
            v, r, w = var[:, 0:n], rstd[:, 0:n], newton[:, 0:n]
            for i in range(NEWTON):
                k = base + 2 * n + 2 + 4 * i
                eng.wait_ge(chain, k)
                ops.tensor_tensor(w, r, r, ALU.mult).then_inc(chain, 1)
                eng.wait_ge(chain, k + 1)
                ops.tensor_tensor(w, w, v, ALU.mult).then_inc(chain, 1)
                eng.wait_ge(chain, k + 2)
                eng.sem_inc(passed, 1)
                ops.tensor_scalar(w, w, -0.5, 1.5, ALU.mult, ALU.add).then_inc(chain, 1)
                eng.wait_ge(chain, k + 3)
                ops.tensor_tensor(r, r, w, ALU.mult).then_inc(chain, 1)

        def centre(dst, src, t, ts):
            return nc.vector.tensor_scalar(dst[:, t, :], src[:, ts, :], moments[:, t, 0:1], rstd[:, t:t + 1],
                                           ALU.subtract, ALU.mult)

        def norm_steps(dve, p, H, b, chain, places, normed):
            stat, aggr, newt, cent = places
            for n in range(NB):
                for j in range(2):
                    if p == stat[n] + j:
                        for t in range(n * TB + 2 * j, n * TB + 2 * j + 2):
                            nc.vector.bn_stats(stats[:, t, :], h[:, b * QT + t, :]).then_inc(chain, 1)
            if p == aggr:
                statistics(dve, chain, H * LN_OPS, h, b * QT, QT, EPS_LAYER, (2,))
            if p == newt:
                first_root(dve, chain, H * LN_OPS, QT, EPS_LAYER)
            for n in range(NB):
                for j in range(2):
                    if p == cent[n][j]:
                        if n == 0 and j == 0:
                            dve.wait_ge(chain, (H + 1) * LN_OPS)
                        for t in range(n * TB + 2 * j, n * TB + 2 * j + 2):
                            last = centre(centred, h, t, b * QT + t)
                        if j == 1:
                            last.then_inc(normed, 1)

        def a_dve(dve, p, H, b, layer):
            norm_steps(dve, p, H, b, ln_a, (A_STATS, A_AGGR, A_NEWTON, A_CENTRE), a_normed)
            if p == A_NEWTON:
                dve.wait_ge(wa_in, (layer + 1) * N_WA)
                nc.vector.tensor_tensor(va[:, 7:8], va[:, 3:4], va[:, 4:5], ALU.add).then_inc(bias_sum, 1)
                dve.wait_ge(bias_sum, H + 1)
                for n in range(NB):
                    dve.wait_ge(a_pool[n], H * A_POOL + 1)
            for n in range(NB):
                tok = slice(n * BLK, (n + 1) * BLK)
                if p == A_BLOCK[n] + 2:
                    dve.wait_ge(a_act, H * A_ACT + 4 * n + 2)
                    nc.vector.scalar_tensor_tensor(work[:, n, 2, :], work[:, n, 0, :], va[:, 2:3], rot[:, 0, tok],
                                                   ALU.add, ALU.mult).then_inc(a_turned, 1)
                    dve.wait_ge(a_ready, H * A_USES + 5 * n + 3)
                    nc.vector.scalar_tensor_tensor(work[:, n, 3, :], bank_proj[:, :], va[:, 7:8],
                                                   rot[:, 1, tok], ALU.add, ALU.mult).then_inc(a_second, 1)
                for k in range(3):
                    if p != A_BLOCK[n] + A_SUBS[k]:
                        continue
                    if k == 0:
                        dve.wait_ge(a_turned, H * NB + n + 1)
                        dve.wait_ge(a_second, H * A_DVE + n + 1)
                        out, y, op = work[:, n, 2, :], work[:, n, 3, :], ALU.add
                    else:
                        what, src = PARTS[k - 1]
                        dve.wait_ge(a_split[n], H * A_SPLIT + k)
                        out, y, op = work[:, n, src, :], split[:, n, 0, what, :], ALU.subtract
                    nc.vector.tensor_tensor(out, out, y, op).then_inc(a_sub[n], 1)
                if p == A_BLOCK[n] + A_COPIES[0]:
                    if n == 0:
                        dve.wait_ge(split_out, H * (16 * 3 * NB) + 16)
                    dve.wait_ge(a_sub[n], H * A_SUB + 1)
                    nc.vector.tensor_copy(split[:, n, 0, 1, :], work[:, n, 2, :]).then_inc(a_parts[n], 1)
                if p == A_BLOCK[n] + A_COPIES[1]:
                    dve.wait_ge(a_sub[n], H * A_SUB + 3)
                    nc.vector.tensor_copy(split[:, n, 1, 2, :], work[:, n, 1, :]).then_inc(a_parts[n], 1)
                if p == A_BLOCK[n] + A_COPIES[2]:
                    dve.wait_ge(a_pool[n], H * A_POOL + 2)
                    nc.vector.tensor_copy(split[:, n, 1, 1, :], work[:, n, 2, :]).then_inc(a_parts[n], 1)

        def a_pe(pe, p, H, b, layer, first=False):
            for n in range(NB):
                j = p - A_BLOCK[n]
                if not 0 <= j < 5:
                    continue
                if j == 3:
                    pe.wait_ge(a_second, H * A_DVE + n + 1)
                elif j > 0 or n > 0:
                    pe.wait_ge(a_act, H * A_ACT + 4 * n + (0, 1, 2, 0, 3)[j])
                elif not first:
                    pe.wait_ge(d_dve, (H - 1) * D_DVE)
                if j == 0:
                    pe.wait_ge(a_normed, H * NB + n + 1)
                    for t in range(TB):
                        last = nc.tensor.transpose(bank_proj[:, t * P:(t + 1) * P], centred[:, n * TB + t, :],
                                                   ident[:, :])
                elif j < 4:
                    if j == 1 and n == 0:
                        pe.wait_ge(wa_in, (layer + 1) * N_WA)
                    last = nc.tensor.matmul(bank_proj[:, :], wa[:, j - 1, :], xn_t[:, n * BLK:(n + 1) * BLK],
                                            start=True, stop=True)
                else:
                    for t in range(TB):
                        tt = n * TB + t
                        last = nc.tensor.matmul(bank_proj[:, t * P:(t + 1) * P], xn_t[:, tt * P:(tt + 1) * P],
                                                wa[:, 3, :], start=True, stop=True)
                last.then_inc(a_ready, 1)

        PARTS = ((0, 0), (2, 1), (1, 2))

        def a_act_steps(act, p, H, b, layer):
            for n in range(NB):
                j = p - A_BLOCK[n]
                if 0 <= j < 5 and j != 2:
                    if n == 0 and j == 0:
                        act.wait_ge(wa_in, (layer + 1) * N_WA)
                    if j == 0:
                        act.wait_ge(a_pool[n], H * A_POOL + 1)
                    act.wait_ge(a_ready, H * A_USES + 5 * n + j + 1)
                    if j == 0:
                        nc.scalar.activation(xn_t[:, n * BLK:(n + 1) * BLK], bank_proj[:, :], ACT.Identity,
                                             bias=va[:, 6:7], scale=va[:, 5:6]).then_inc(a_act, 1)
                    elif j == 4:
                        nc.scalar.activation(values[:, b, n * TB:(n + 1) * TB, :, 0:DH],
                                             bank_proj[:, :].rearrange("p (t h d) -> p t h d", t=TB, d=DH),
                                             ACT.Copy).then_inc(a_act, 1)
                    else:
                        i = (j - 1) // 2
                        nc.scalar.activation(work[:, n, i, :], bank_proj[:, :], ACT.Identity, bias=va[:, i:i + 1])\
                          .then_inc(a_act, 1)
                for i, (what, src) in enumerate(PARTS[:2]):
                    if j == A_HIGH[i]:
                        if n == 0 and i == 0:
                            act.wait_ge(split_out, H * (16 * 3 * NB) + 16)
                        act.wait_ge(a_act, H * A_ACT + 4 * n + 2 + i)
                        nc.scalar.activation(split[:, n, 0, what, :], work[:, n, src, :], ACT.Copy)\
                          .then_inc(a_split[n], 1)
                if j == A_MIDDLE:
                    act.wait_ge(a_sub[n], H * A_SUB + 2)
                    nc.scalar.activation(split[:, n, 1, 0, :], work[:, n, 0, :], ACT.Copy).then_inc(a_split[n], 1)

        def a_pool_steps(pool, p, H, b):
            if p == A_NEWTON:
                newton_steps(pool, nc.gpsimd, ln_a, H * LN_OPS, QT)
            for n in range(NB):
                j = p - A_BLOCK[n]
                for k in range(4):
                    if j != A_ADDS[k]:
                        continue
                    low = k > 0
                    what, src = PARTS[k - 1 if low else 2]
                    if what == 0:
                        pool.wait_ge(a_split[n], (H + 1) * A_SPLIT)
                    else:
                        pool.wait_ge(a_parts[n], H * A_PARTS + (1, 0, 2, 3)[k])
                    x, y, op = work[:, n, src, :], split[:, n, int(low), what, :], ALU.subtract
                    out = split[:, n, 2, what, :] if low else x
                    nc.gpsimd.tensor_tensor(out, x, y, op).then_inc(a_pool[n], 1)

        def d_pe(pe, p, H, b, layer, last_half=False):
            for n in range(NB):
                tok = slice(n * TB, (n + 1) * TB)
                if p == D_CONTEXT[n]:
                    if n == 0:
                        if last_half:
                            pe.wait_ge(d_dve, H * D_DVE)
                        else:
                            pe.wait_ge(a_act, (H + 2) * A_ACT - A_ACT)
                        pe.wait_ge(small_read, n_small(H * NQ + NQ - 1, 2) - last_half)
                        pe.wait_ge(wd_in, (layer + 1) * N_WD)
                    else:
                        pe.wait_ge(d_act, H * D_ACT + n)
                    for t in range(TB):
                        last = nc.tensor.transpose(bank_proj[:, t * P:(t + 1) * P],
                                                   context[:, n * TB + t, :, :].rearrange("p h d -> p (h d)"),
                                                   ident[:, :])
                    last.then_inc(d_ready, 1)
                if p == D_WO[n]:
                    pe.wait_ge(d_act, H * D_ACT + NB)
                    if n:
                        pe.wait_ge(d_dve, H * D_DVE + n)
                    for t in range(TB):
                        tt = n * TB + t
                        last = nc.tensor.matmul(bank_proj[:, t * P:(t + 1) * P], d_t[:, tt * P:(tt + 1) * P],
                                                wo[:, :], start=True, stop=True)
                    last.then_inc(d_ready, 1)
                if p == D_TURN[n]:
                    pe.wait_ge(d_normed, H * NB + n + 1)
                    if n:
                        pe.wait_ge(d_act, H * D_ACT + 3)
                    else:
                        pe.wait_ge(d_dve, H * D_DVE + 2)
                    for t in range(TB):
                        last = nc.tensor.transpose(bank_proj[:, t * P:(t + 1) * P], centred[:, n * TB + t, :],
                                                   ident[:, :])
                    last.then_inc(d_ready, 1)
                f = p - D_UP[n]
                if 0 <= f < FT:
                    pe.wait_ge(d_act, H * D_ACT + 4 + FT * n + f)
                    nc.tensor.matmul(bank_proj[:, :], w1[:, f * P:(f + 1) * P], d_t[:, n * BLK:(n + 1) * BLK],
                                     start=True, stop=True).then_inc(d_ready, 1)
                for t in range(TB):
                    if p != D_DOWN[n][t]:
                        continue
                    if t == 0:
                        pe.wait_ge(d_gelu, H * NB + n + 1)
                        if n:
                            pe.wait_ge(d_dve, H * D_DVE + 3)
                    for f in range(FT):
                        last = nc.tensor.matmul(bank_proj[:, t * P:(t + 1) * P], (inner_last if last_half else inner)[n][:, f, t * P:(t + 1) * P],
                                                w2[:, f, :], start=f == 0, stop=f == FT - 1)
                    if t == TB - 1:
                        last.then_inc(d_ready, 1)

        def d_act_steps(act, p, H, b, layer, last_half=False):
            values_in = inner_last if last_half else inner
            for n in range(NB):
                blk = slice(n * BLK, (n + 1) * BLK)
                if p == D_CONTEXT[n]:
                    if n == 0:
                        act.wait_ge(wd_in, (layer + 1) * N_WD)
                    act.wait_ge(d_ready, H * D_USES + n + 1)
                    nc.scalar.activation(d_t[:, blk], bank_proj[:, :], ACT.Identity, bias=vd[:, 0:1])\
                      .then_inc(d_act, 1)
                if p == D_TURN[n]:
                    act.wait_ge(d_ready, H * D_USES + 5 + n)
                    nc.scalar.activation(d_t[:, blk], bank_proj[:, :], ACT.Identity, bias=vd[:, 2:3],
                                         scale=vd[:, 1:2]).then_inc(d_act, 1)
                f = p - D_UP[n]
                if 0 <= f < FT:
                    act.wait_ge(d_ready, H * D_USES + 7 + FT * n + f)
                    nc.scalar.activation(values_in[n][:, f, :], bank_proj[:, :], ACT.Identity, bias=vd[:, 3 + f:4 + f])\
                      .then_inc(d_act, 1)
                if p == D_GELU:
                    act.wait_ge(d_act, H * D_ACT + 4 + FT * NB)
                    nc.scalar.activation(values_in[n][:, :, :], values_in[n][:, :, :], ACT.Gelu).then_inc(d_gelu, 1)

        def d_dve_steps(dve, p, H, b):
            def add_in(n):
                dst = h[:, b * QT + n * TB:b * QT + (n + 1) * TB, :]
                nc.vector.tensor_tensor(dst, dst, bank_proj[:, :].rearrange("p (t c) -> p t c", t=TB), ALU.add)\
                  .then_inc(d_dve, 1)

            for n in range(NB):
                if p == D_WO[n]:
                    dve.wait_ge(bias_added, H * 2 * NB + n + 1)
                    dve.wait_ge(d_ready, H * D_USES + 3 + n)
                    add_in(n)
                if p == D_STATS[n]:
                    dve.wait_ge(d_dve, H * D_DVE + n + 1)
                if p == D_DOWN[n][TB - 1]:
                    dve.wait_ge(bias_added, H * 2 * NB + NB + n + 1)
                    dve.wait_ge(d_ready, H * D_USES + 7 + FT * NB + n)
                    add_in(n)
                if p == A_STATS[n]:
                    dve.wait_ge(d_dve, H * D_DVE + NB + n + 1)
            norm_steps(dve, p, H, b, ln_d, (D_STATS, D_AGGR, D_NEWTON, D_CENTRE), d_normed)

        def d_pool_steps(pool, p, H, b, layer):
            if p == D_NEWTON:
                newton_steps(pool, nc.gpsimd, ln_d, H * LN_OPS, QT)
            for i, places in enumerate((D_ROW, D_ROW2)):
                for n in range(NB):
                    if p == places[n]:
                        if i == 0 and n == 0:
                            pool.wait_ge(wd_in, (layer + 1) * N_WD)
                        if i == 0:
                            pool.wait_ge(a_normed, H * NB + NB)
                        else:
                            pool.wait_ge(d_normed, H * NB + NB)
                        dst = h[:, b * QT + n * TB:b * QT + (n + 1) * TB, :]
                        nc.gpsimd.tensor_tensor(dst, dst, rows[:, i:i + 1, :].broadcast_to((P, TB, D)), ALU.add)\
                          .then_inc(bias_added, 1)

        def slot_of(v_rel):
            quad, c = divmod(v_rel, NU)
            return quad % NQ, quad % 2, c

        def pe_pass1(pe, H, v_rel):
            s, par, c = slot_of(v_rel)
            qt, k0, n = CHUNKS[c]
            v = H * (NQ * NU) + v_rel
            if c == 0:
                pe.wait_ge(stack_in[s], (H + v_rel // NU // NQ + 1) * N_STACK + 16)
            return [(g, qt, k0, n, v, s) for g in range(G)]

        def pe_pass1_one(pe, item):
            g, qt, k0, n, v, s = item
            pe.wait_ge(max_done, n_max_done(v, g) - 2)
            has_diagonal = k0 + n == (qt + 1) * P
            mm = nc.tensor.matmul(bank_max[g % 2][:, 0:n], q_stack[0:SHIFT, s, g, qt * P:(qt + 1) * P],
                                  k_stack[0:SHIFT, s, g, k0:k0 + n], start=True, stop=not has_diagonal)
            if has_diagonal:
                mm = nc.tensor.matmul(bank_max[g % 2][:, n - P:n], ident_b[:, :], mask_b[:, :],
                                      start=False, stop=True)
            mm.then_inc(max_ready, 1)

        def dve_pass1(dve, H, v_rel, midway=None):
            s, par, c = slot_of(v_rel)
            qt, k0, n = CHUNKS[c]
            v = H * (NQ * NU) + v_rel
            dst = top if k0 == 0 else top2
            for g in range(G):
                dve.wait_ge(max_ready, n_max(v, g))
                nc.vector.reduce_max(dst[:, par, g, qt:qt + 1], bank_max[g % 2][:, 0:n], AX.X).then_inc(max_done, 1)
                if g == 1 and midway:
                    midway()
            if c == NU - 1:
                dve.wait_ge(max_done, n_max_done(v, G - 1))
                nc.vector.tensor_tensor(top[:, par, :, TB:QT], top[:, par, :, TB:QT], top2[:, par, :, TB:QT], ALU.max)\
                  .then_inc(merged, 1)

        def pe_top(pe, q, par, small):
            pe.wait_ge(merged, q + 1)
            if small is not None:
                pe.wait_ge(small_read, small - 1)
            nc.tensor.transpose(bank_small[0:G * QT, 0:P], top[:, par, :, :].rearrange("p g t -> p (g t)"),
                                ident[:, :]).then_inc(small_ready, 1)

        def dve_top(dve, q, par, small):
            dve.wait_ge(small_ready, small)
            if q is not None:
                dve.wait_ge(neg_done, q * 2)
            dst = neg_top[:, par, :, :]
            nc.vector.tensor_scalar(dst[:, 0, :], bank_small[0:G * QT, 0:P], -1.0, None, ALU.mult).then_inc(neg_done, 1)
            qq = 0 if q is None else q
            dve.wait_ge(neg_done, qq * 2 + 1)
            nc.vector.scalar_tensor_tensor(dst[:, 1, :], bank_small[0:G * QT, 0:P], -1.0, dst[:, 0, :], ALU.mult,
                                           ALU.subtract).then_inc(neg_done, 1)
            dve.wait_ge(neg_done, qq * 2 + 2)
            dve.sem_inc(small_read, 1)

        def score_bank(wide, g):
            return (bank_score + bank_max)[g] if wide else bank_score[g % 2]

        def pe_scores(pe, H, s, u, wide):
            b, t = UNITS[u]
            first, n = span(u)
            q = H * NQ + s
            if u == 0:
                pe.wait_ge(shift_in[s], (H + 1) * 32 + (16 if s == NQ - 1 else 0))
            return [(q, s, u, g, t, b * BLK + first, n, wide) for g in range(G)]

        def pe_score_one(pe, item):
            q, s, u, g, t, q0, n, wide = item
            before = G if wide and u > 0 else 2
            if not (wide and u == 0 and g >= 2):
                pe.wait_ge(exp_done, n_exp(q, u, g) - before)
            nc.tensor.matmul(score_bank(wide, g)[:, 0:n], k_stack[0:ROWS, s, g, t * P:(t + 1) * P],
                             q_stack[0:ROWS, s, g, q0:q0 + n], start=True, stop=True).then_inc(score_ready, 1)

        def act_exps(act, H, s, u, midway, wide):
            first, n = span(u)
            q = H * NQ + s
            act.wait_ge(pv_done, n_pv(q, u) - RING)
            for g in range(G):
                act.wait_ge(score_ready, n_score(q, u, g))
                nc.scalar.activation(probs[:, u % RING, g, 0:n], score_bank(wide, g)[:, 0:n], ACT.Exp, scale=SCALE)\
                  .then_inc(exp_done, 1)
                if g == 1:
                    midway()

        def pool_mask(pool, H, s, u):
            q = H * NQ + s
            pool.wait_ge(exp_done, n_exp(q, u, G - 1))
            pool.sem_inc(passed, 1)
            tile = probs[:, u % RING, :, 0:P]
            nc.gpsimd.affine_select(out=tile, in_=tile, compare_op=ALU.is_ge, fill=0.0, base=0,
                                    pattern=[[0, G], [1, P]], channel_multiplier=-1).then_inc(mask_done, 1)

        def pe_pv(pe, q, b, s, u, halves=(0, 1)):
            blk, t = UNITS[u]
            first, n = span(u)
            cut = n // 2 if n > WHOLE else 0
            if 0 in halves and cut or 1 in halves and not cut:
                if diagonal(u):
                    pe.wait_ge(mask_done, n_mask(q, u))
                else:
                    pe.wait_ge(exp_done, n_exp(q, u, G - 1))
                if u == FIRST_OF[blk]:
                    pe.wait_ge(pv_read, n_pv_read(q - 1, blk))
            for i, (lo, hi) in enumerate(((0, cut), (cut, n))):
                if i not in halves or lo == hi:
                    continue
                for g in range(G):
                    last = nc.tensor.matmul(bank_pv[blk][32 * g:32 * g + V_COLS, first + lo:first + hi],
                                            values[:, b, t, s * G + g, :], probs[:, u % RING, g, lo:hi],
                                            start=u == FIRST_OF[blk] and lo == 0,
                                            stop=u == LAST_OF[blk] and hi == n)
                if i == 1:
                    last.then_inc(pv_done, 1)

        def act_pv_out(act, q, blk):
            act.wait_ge(pv_done, n_pv(q, LAST_OF[blk]))
            act.wait_ge(small_ready, n_small(q - 1, 2 * blk))
            nc.scalar.activation(context_raw[:, blk, :], bank_pv[blk][:, :], ACT.Copy).then_inc(pv_read, 1)

        def pe_tail(pe, q, blk, before):
            pe.wait_ge(pv_read, n_pv_read(q, blk))
            pe.wait_ge(small_read, before)
            for t in range(TB):
                last = nc.tensor.transpose(bank_small[:, t * P:(t + 1) * P], context_raw[:, blk, t * P:(t + 1) * P],
                                           ident[:, :])
            last.then_inc(small_ready, 1)

        def dve_tail(dve, q, s, blk, ready):
            dve.wait_ge(small_ready, ready)
            got = bank_small[:, :].rearrange("p (t g c) -> p t g c", t=TB, g=G)
            nc.vector.reciprocal(rden[:, :, :], got[:, :, :, DH]).then_inc(rden_done, 1)
            dve.wait_ge(rden_done, q * NB + blk + 1)
            nc.vector.tensor_tensor(context[:, blk * TB:(blk + 1) * TB, s * G:(s + 1) * G, :], got[:, :, :, 0:DH],
                                    rden[:, :, :].unsqueeze(3).broadcast_to((P, TB, G, DH)), ALU.mult)\
              .then_inc(small_read, 1)

        N_X = B * (LN_OPS + QT)

        def f_pe(pe, p, fb):
            def last_of(products):
                for last in products:
                    pass
                return last

            for n in range(NB):
                tiles = [(t, fb * QT + n * TB + t) for t in range(TB)]
                if p == F_TURN[n]:
                    pe.wait_ge(x_normed, NB * fb + n + 1)
                    if n:
                        pe.wait_ge(xt_read, NB * fb + n)
                    last_of(nc.tensor.transpose(bank_proj[:, t * P:(t + 1) * P], acc[:, tt, :], ident[:, :])
                            for t, tt in tiles).then_inc(xt_ready, 1)
                if p == F_GATES[n]:
                    pe.wait_ge(router, (fb + 1) * ROUTER_STEPS)
                    if n:
                        pe.wait_ge(gates_read, NB * fb + n)
                    last_of(nc.tensor.transpose(bank_proj[0:EXPERTS, t * P:(t + 1) * P], gates[:, tt, :],
                                                ident[:, :]) for t, tt in tiles).then_inc(gates_ready, 1)
                if p == F_B2[n]:
                    pe.wait_ge(gates_read, NB * (fb + 1))
                    if n:
                        pe.wait_ge(b2_read, NB * fb + n)
                    last_of(nc.tensor.matmul(bank_proj[:, t * P:(t + 1) * P], gates_t[:, tt * P:(tt + 1) * P],
                                             b2_rows[:, :], start=True, stop=True)
                            for t, tt in tiles).then_inc(b2_ready, 1)
            if p == F_ROUTER:
                pe.wait_ge(xt_read, NB * (fb + 1))
                last_of(nc.tensor.matmul(bank_proj[:, t * E:(t + 1) * E],
                                         x2_t[:, (fb * QT + t) * P:(fb * QT + t + 1) * P], wr[:, :],
                                         start=True, stop=True) for t in range(QT)).then_inc(router_done, 1)

        def f_act(act, p, fb):
            for n in range(NB):
                m = NB * fb + n
                blk = slice(m * BLK, (m + 1) * BLK)
                if p == F_TURN[n]:
                    if m == 0:
                        for a in a_pool:
                            act.wait_ge(a, 2 * L * A_POOL + 1)
                    act.wait_ge(xt_ready, m + 1)
                    nc.scalar.activation(x2_t[:, blk], bank_proj[:, :], ACT.Copy).then_inc(xt_read, 1)
                if p == F_GATES[n]:
                    act.wait_ge(gates_ready, m + 1)
                    nc.scalar.activation(gates_t[:, blk], bank_proj[0:EXPERTS, :], ACT.Copy).then_inc(gates_read, 1)
                if p == F_B2[n]:
                    act.wait_ge(b2_ready, m + 1)
                    nc.scalar.activation(acc[:, m * TB:(m + 1) * TB, :],
                                         bank_proj[:, :].rearrange("p (t c) -> p t c", t=TB), ACT.Copy)\
                      .then_inc(b2_read, 1)
            if p == F_CHAIN + 2:
                act.wait_ge(router, fb * ROUTER_STEPS + 2)
                mine = slice(fb * QT, (fb + 1) * QT)
                nc.scalar.activation(prob_e[:, mine, :], logit[:, mine, :], ACT.Exp).then_inc(router_exp, 1)

        def f_dve(dve, p, fb):
            base = N_X + fb * (1 + LN_OPS)
            mine = slice(fb * QT, (fb + 1) * QT)
            if p == F_ADD:
                dve.wait_ge(x_again_in, 16)
                dve.wait_ge(d_dve, (LAST + fb) * D_DVE)
                nc.vector.tensor_tensor(h[:, mine, :], h[:, mine, :], x_again[:, mine, :], ALU.add).then_inc(ln_x, 1)
            if p == F_STATS[0]:
                dve.wait_ge(ln_x, base + 1)
            stages = [i for i, at in enumerate((*F_STATS, F_AGGR, F_ROOT)) if p == at]
            if stages:
                statistics(dve, ln_x, base + 1, h, fb * QT, QT, EPS_OUT, stages)
            if 0 <= p - F_CENTRE < 4:
                if p == F_CENTRE:
                    dve.wait_ge(ln_x, base + 1 + LN_OPS)
                for t in range(2 * (p - F_CENTRE), 2 * (p - F_CENTRE) + 2):
                    last = nc.vector.tensor_scalar(acc[:, fb * QT + t, :], h[:, fb * QT + t, :],
                                                   moments[:, t, 0:1], rstd[:, t:t + 1], ALU.subtract, ALU.mult)
                if (p - F_CENTRE) % 2:
                    last.then_inc(x_normed, 1)
            k = p - F_CHAIN
            if 0 <= k < ROUTER_STEPS:
                if k == 0:
                    dve.wait_ge(router_done, fb + 1)
                else:
                    dve.wait_ge(router, fb * ROUTER_STEPS + k)
                if k == 2:
                    dve.wait_ge(router_exp, fb + 1)
                router_step(k, mine).then_inc(router, 1)

        def router_step(k, mine):
            got = bank_proj[:, 0:QT * E].rearrange("p (t e) -> p t e", e=E)
            wide = one_col[:, mine].unsqueeze(2).broadcast_to((P, QT, E))
            pr, rk, cm = prob_e[:, mine, :], rank[:, mine, :], cmp[:, mine, :]
            if k == 0:
                return nc.vector.tensor_reduce(one_col[:, mine], got, AX.X, ALU.max)
            if k == 1:
                return nc.vector.tensor_tensor(logit[:, mine, :], got, wide, ALU.subtract)
            if k == 2:
                return nc.vector.tensor_reduce(one_col[:, mine], pr, AX.X, ALU.add)
            if k == 3:
                return nc.vector.reciprocal(one_col[:, mine], one_col[:, mine])
            if k == 4:
                return nc.vector.tensor_tensor(pr, pr, wide, ALU.mult)
            o, part = divmod(k - 5, 3)
            if o < E:
                other = prob_e[:, mine, o:o + 1]
                if part == 0 and o == 0:
                    return nc.vector.memset(rk, 0.0)
                if part == 0:
                    return nc.vector.tensor_tensor(cmp[:, mine, 0:o], other.broadcast_to((P, QT, o)),
                                                   prob_e[:, mine, 0:o], ALU.is_gt)
                if part == 1:
                    return nc.vector.tensor_tensor(cmp[:, mine, o:E], other.broadcast_to((P, QT, E - o)),
                                                   prob_e[:, mine, o:E], ALU.is_ge)
                return nc.vector.tensor_tensor(rk, rk, cm, ALU.add)
            if part == 0:
                return nc.vector.tensor_scalar(cm, rk, 2.5, None, ALU.is_lt)
            if part == 1:
                return nc.vector.tensor_tensor(gates[:, mine, 0:E], cm, pr, ALU.mult)
            return nc.vector.tensor_copy(gates_e[:, 0:E, mine], gates[:, mine, 0:E].rearrange("p t e -> p e t"))

        up_banks = [bank_score[0], bank_score[1], bank_max[0], bank_max[1]]
        down_banks = bank_pv
        FIRST_TILES = [(0, 0), (0, 1), (1, 0), (1, 1), (0, 2), (0, 3), (1, 2), (1, 3)]

        def up(pe, k, par, n):
            for f in range(FT):
                pe.wait_ge(gelu_done, k * FT + f + 1)
                nc.tensor.matmul(up_banks[f][:, :], we[:, par, f * P:(f + 1) * P],
                                 x2_t[:, n * BLK:(n + 1) * BLK], start=True, stop=True).then_inc(up_ready, 1)

        def gelu(act, k, par, n):
            act.wait_ge(down_ready, k + 1)
            for f in range(FT):
                act.wait_ge(up_ready, k * FT + f + 1)
                nc.scalar.activation(probs[:, 2 + n % 2, f, :], up_banks[f][:, :], ACT.Gelu_apprx_tanh,
                                     bias=b1_now[:, par, f:f + 1]).then_inc(gelu_done, 1)

        def down(pe, k, par, n):
            pe.wait_ge(gelu_done, k * FT + FT + 4)
            pe.wait_ge(acc_done, k + 1)
            for t in range(TB):
                for f in range(FT):
                    last = nc.tensor.matmul(down_banks[n % 2][:, t * P:(t + 1) * P],
                                            probs[:, 2 + n % 2, f, t * P:(t + 1) * P],
                                            we[:, par, FF + f * D:FF + (f + 1) * D],
                                            start=f == 0, stop=f == FT - 1)
            last.then_inc(down_ready, 1)

        def add_up(dve, k, par, n):
            dve.wait_ge(down_ready, k + 3)
            for t in range(TB):
                tt = n * TB + t
                last = nc.vector.scalar_tensor_tensor(acc[:, tt, :], down_banks[n % 2][:, t * P:(t + 1) * P],
                                                      gate_now[:, par, tt:tt + 1], acc[:, tt, :], ALU.mult, ALU.add)
            last.then_inc(acc_done, 1)

        RAW0, TAIL0, TOP, RAW1, TAIL1 = 6, 8, 9, 2, 3

        def v_exists(more, v_rel):
            return more or v_rel < NQ * NU

        def pe_half(pe, H, b, layers, before=True, more=True):
            def place(p):
                if before:
                    d_pe(pe, p, H - 1, 1 - b, layers[0])
                if more:
                    a_pe(pe, p, H + 1, 1 - b, layers[2])
                else:
                    f_pe(pe, p, 0)

            for s in range(NQ):
                for u in range(NU):
                    q = H * NQ + s
                    scores = pe_scores(pe, H, s, u, not more and s == NQ - 1)
                    v_rel = s * NU + u + AHEAD
                    maxes = pe_pass1(pe, H, v_rel) if v_exists(more, v_rel) else [None] * G
                    def pv(half):
                        if u >= LAG:
                            pe_pv(pe, q, b, s, u - LAG, half)
                        elif s > 0 or before:
                            pe_pv(pe, q - 1, b if s else 1 - b, (s - 1) % NQ, u - LAG + NU, half)

                    late = before and 2 * (s * NU + u) == D_GELU + 1
                    for g, (a, m) in enumerate(zip(scores, maxes)):
                        if not late or g < 2:
                            pe_score_one(pe, a)
                        if m:
                            pe_pass1_one(pe, m)
                        if g == 1:
                            pv((0,))
                            place(2 * (s * NU + u))
                    pv((1,))
                    if late:
                        place(2 * (s * NU + u) + 1)
                        pe_score_one(pe, scores[2])
                        pe_score_one(pe, scores[3])
                    if u == TAIL0:
                        pe_tail(pe, q, 0, n_small(q, 0) - 1)
                    if u == TOP and (more or s < NQ - 1):
                        pe_top(pe, q + 1, (s + 1) % 2, n_small(q, 1))
                    if u == TAIL1 and (s > 0 or before):
                        pe_tail(pe, q - 1, 1, n_small(q - 1, 2) - 1)
                    if not late:
                        place(2 * (s * NU + u) + 1)

        def act_half(act, H, b, layers, before=True, more=True):
            def place(p):
                if before:
                    d_act_steps(act, p, H - 1, 1 - b, layers[0])
                if more:
                    a_act_steps(act, p, H + 1, 1 - b, layers[2])
                else:
                    f_act(act, p, 0)

            for s in range(NQ):
                for u in range(NU):
                    q = H * NQ + s
                    act_exps(act, H, s, u, lambda: place(2 * (s * NU + u)), not more and s == NQ - 1)
                    if u == RAW0:
                        act_pv_out(act, q, 0)
                    if u == RAW1 and (s > 0 or before):
                        act_pv_out(act, q - 1, 1)
                    place(2 * (s * NU + u) + 1)

        def dve_half(dve, H, b, layers, before=True, more=True):
            def place(p):
                if before:
                    d_dve_steps(dve, p, H - 1, 1 - b)
                if more:
                    a_dve(dve, p, H + 1, 1 - b, layers[2])
                else:
                    f_dve(dve, p, 0)

            for s in range(NQ):
                for u in range(NU):
                    q = H * NQ + s
                    v_rel = s * NU + u + AHEAD
                    if v_exists(more, v_rel):
                        dve_pass1(dve, H, v_rel, lambda: place(2 * (s * NU + u)))
                    else:
                        place(2 * (s * NU + u))
                    if u == TAIL0:
                        dve_tail(dve, q, s, 0, n_small(q, 0))
                    if u == TOP and (more or s < NQ - 1):
                        dve.wait_ge(shift_in[(s - 1) % NQ], (H + 1) * 32 if s > 0 else H * 32 + 16)
                        dve_top(dve, q + 1, (s + 1) % 2, n_small(q, 1))
                    if u == TAIL1 and (s > 0 or before):
                        dve_tail(dve, q - 1, (s - 1) % NQ, 1, n_small(q - 1, 2))
                    place(2 * (s * NU + u) + 1)

        def pool_half(pool, H, b, layers, before=True, more=True):
            def place(p):
                if before:
                    d_pool_steps(pool, p, H - 1, 1 - b, layers[0])
                if more:
                    a_pool_steps(pool, p, H + 1, 1 - b)

            for s in range(NQ):
                for u in range(NU):
                    place(2 * (s * NU + u))
                    if diagonal(u):
                        pool_mask(pool, H, s, u)
                    place(2 * (s * NU + u) + 1)

        def run_halves(eng, half):
            half(eng, 0, 0, (0, 0, 0), before=False)
            with eng.Fori(0, L - 1) as l:
                half(eng, l * 2 + 1, 1, (l, l, l + 1))
                half(eng, l * 2 + 2, 0, (l, l + 1, l + 1))
            half(eng, 2 * L - 1, 1, (L - 1, L - 1, L - 1), more=False)

        LAST = 2 * L - 1
        LAST_Q = 2 * L * NQ - 1

        INIT = 5
        N_CONST = 16 * (7 + NQ * G)
        WE = 2 * FF

        block = ctx.enter_context(nc.Block())

        @block.sync
        def _(sp):
            sp.dma_start(h[:, 0:QT, :], xv[:, 0:QT, :]).then_inc(x_in[0], 16)
            load_a_weights(sp, 0)
            sp.sem_inc(split_out, 16)
            for s in range(NQ):
                sp.sem_inc(stack_in[s], 16)
            sp.sem_inc(shift_in[NQ - 1], 16)
            for dst, src in ((ident[:, :], ident_d), (ident_b[:, :], identb_d), (mask_b[:, :], maskb_d),
                             (rot[:, :, :], rot_d), (wr[:, :], wr_d), (b2_rows[:, :], be_d[:, 0:D]),
                             (be[:, :, :], be_d[:, D:D + FF].rearrange("e (p f) -> p e f", p=P))):
                sp.dma_start(dst, src).then_inc(const_in, 16)
            for s in range(NQ):
                for g in range(G):
                    sp.dma_start(k_stack[REL:ROWS, s, g, :], kst_d).then_inc(const_in, 16)
            sp.dma_start(h[:, QT:NT, :], xv[:, QT:NT, :]).then_inc(x_in[1], 16)
            load_d_weights(sp, 0)
            store_split(sp, (0, 0))
            for s in range(NQ):
                load_stacks(sp, (0, 0), s)
            load_shift(sp, 0, 0, 0)

            def half(sp, H, b, layers, before=True, more=True):
                sp_half(sp, H, b, layers[1], before, more)

            run_halves(sp, half)
            for e, tiles in ((0, 6), (1, 8)):
                sp.wait_ge(down_ready, tiles + 2)
                sp.dma_start(we[:, e, :], we_d[e + 2]).then_inc(we_in[e], 16)
            with sp.Fori(1, E // 2 - 1) as i:
                for par in range(2):
                    sp.wait_ge(down_ready, (i * 2 + par + 1) * (NB * B) + 2)
                    sp.sem_inc(passed, 1)
                    sp.dma_start(we[:, par, :], we_d[bass.ds(i * 2 + par + 2, 1)].rearrange("o p n -> (o p) n"))\
                      .then_inc(we_in[par], 16)
            sp.wait_ge(down_ready, (E - 1) * (NB * B) + 2)
            sp.dma_start(we[:, 0, :], we_d[E]).then_inc(we_in[0], 16)
            sp.wait_ge(finished, 1)
            sp.dma_start(out_d.rearrange("b (t p) c -> p (b t) c", p=P), acc[:, :, :]).then_inc(out_done, 16)
            sp.wait_ge(out_done, 16)

        @block.gpsimd
        def _(pool):
            for n in range(NB):
                pool.sem_inc(a_pool[n], 1)
            for p in range(PLACES):
                a_pool_steps(pool, p, 0, 0)
            run_halves(pool, pool_half)
            for p in range(DOWN_AT[-1] + 1):
                d_pool_steps(pool, p, LAST, 1, L - 1)

        @block.scalar
        def _(act):
            act.sem_inc(exp_done, 2)
            act.sem_inc(pv_read, 2)
            for p in range(PLACES):
                a_act_steps(act, p, 0, 0, 0)
            run_halves(act, act_half)
            act_pv_out(act, LAST_Q, 1)
            act.sem_inc(gelu_done, 4)
            act.wait_ge(gate_copied, 2)
            for p in range(DOWN_AT[-1] + 1):
                d_act_steps(act, p, LAST, 1, L - 1, last_half=True)
                for k in range(4):
                    if p == GELU_AT[k]:
                        gelu(act, k, *FIRST_TILES[k])
            for p in range(F_GATES[0]):
                f_act(act, p, 1)
            for k in range(4, 8):
                gelu(act, k, *FIRST_TILES[k])
            for p in range(F_GATES[0], F_PLACES):
                f_act(act, p, 1)

            def expert(e, par):
                for n in range(NB * B):
                    gelu(act, e * 4 + n, par, n)

            with act.Fori(1, E // 2) as i:
                for par in range(2):
                    act.wait_ge(gate_copied, i * 2 + par + 1)
                    expert(i * 2 + par, par)
            act.wait_ge(gate_copied, E + 1)
            expert(E, 0)

        @block.tensor
        def _(pe):
            pe.sem_inc(pv_done, RING)
            pe.sem_inc(small_ready, 2)
            pe.wait_ge(const_in, N_CONST)
            pe.wait_ge(init_done, INIT)
            for p in range(PLACES):
                a_pe(pe, p, 0, 0, 0, first=True)
            for v in range(AHEAD):
                for item in pe_pass1(pe, 0, v):
                    pe_pass1_one(pe, item)
                if v == NU - 1:
                    pe_top(pe, 0, 0, None)
            run_halves(pe, pe_half)
            for u in range(NU - LAG, NU):
                pe_pv(pe, LAST_Q, 1, NQ - 1, u)
            pe.sem_inc(down_ready, 2)
            for par in range(2):
                pe.wait_ge(we_in[par], 16)
            pe_tail(pe, LAST_Q, 1, n_small(LAST_Q, 2) - 2)
            for p in range(DOWN_AT[-1] + 1):
                d_pe(pe, p, LAST, 1, L - 1, last_half=True)
                for k in range(4):
                    if p == UP_AT[k]:
                        up(pe, k, *FIRST_TILES[k])
                    if p == DOWN_AT[k]:
                        down(pe, k, *FIRST_TILES[k])
            for p in range(F_GATES[0]):
                f_pe(pe, p, 1)
            up(pe, 4, *FIRST_TILES[4])
            for k in range(5, 8):
                up(pe, k, *FIRST_TILES[k])
                if k < 7:
                    down(pe, k - 1, *FIRST_TILES[k - 1])
            for p in range(F_GATES[0], F_PLACES):
                f_pe(pe, p, 1)
            for k in range(6, 8):
                down(pe, k, *FIRST_TILES[k])

            def expert(e, par, arrived):
                pe.wait_ge(we_in[par], arrived)
                up(pe, e * 4, par, 0)
                for n in range(1, NB * B):
                    up(pe, e * 4 + n, par, n)
                    down(pe, e * 4 + n - 1, par, n - 1)
                down(pe, e * 4 + NB * B - 1, par, NB * B - 1)

            with pe.Fori(1, E // 2) as i:
                for par in range(2):
                    expert(i * 2 + par, par, i * 16 + 16)
            expert(E, 0, 16 * (E // 2 + 1))

        @block.vector
        def _(dve):
            nc.vector.memset(values[:, :, :, :, DH:V_COLS], 1.0).then_inc(init_done, 1)
            for b in bank_pv:
                nc.vector.memset(b[:, :], 0.0).then_inc(init_done, 1)
            nc.vector.memset(gates[:, :, E:E + 1], 1.0).then_inc(init_done, 1)
            nc.vector.memset(gates_e[:, E, :], 1.0).then_inc(init_done, 1)
            dve.sem_inc(max_done, 2)
            dve.sem_inc(small_read, 2)
            def norm_input(b):
                base = b * (LN_OPS + QT)
                dve.wait_ge(x_in[b], 16)
                statistics(dve, ln_x, base, h, b * QT, QT, EPS_OUT)
                dve.wait_ge(ln_x, base + LN_OPS)
                for t in range(QT):
                    nc.vector.tensor_scalar(h[:, b * QT + t, :], h[:, b * QT + t, :], moments[:, t, 0:1],
                                            rstd[:, t:t + 1], ALU.subtract, ALU.mult).then_inc(ln_x, 1)
                dve.wait_ge(ln_x, base + LN_OPS + QT)

            norm_input(0)
            dve.wait_ge(const_in, N_CONST)
            for p in range(PLACES):
                a_dve(dve, p, 0, 0, 0)
            norm_input(1)
            for v in range(AHEAD):
                dve_pass1(dve, 0, v)
                if v == NU - 1:
                    dve_top(dve, None, 0, 3)
            run_halves(dve, dve_half)
            dve.wait_ge(router, ROUTER_STEPS)
            for e in range(2):
                nc.vector.tensor_copy(b1_now[:, e, :].unsqueeze(1), be[:, e:e + 1, :])
                nc.vector.tensor_copy(gate_now[:, e, 0:QT].unsqueeze(1), gates_e[:, e:e + 1, 0:QT])\
                  .then_inc(gate_copied, 1)
            dve_tail(dve, LAST_Q, NQ - 1, 1, n_small(LAST_Q, 2) - 1)
            dve.sem_inc(acc_done, 2)
            dve.wait_ge(gate_copied, 2)
            dve.wait_ge(b2_read, NB)
            for p in range(DOWN_AT[-1] + 1):
                d_dve_steps(dve, p, LAST, 1)
                for k in range(4):
                    if k < len(ACC_AT) and p == ACC_AT[k]:
                        add_up(dve, k, *FIRST_TILES[k])
            for p in range(F_PLACES):
                if p == F_TURN[0]:
                    add_up(dve, 3, *FIRST_TILES[3])
                f_dve(dve, p, 1)
            dve.wait_ge(router, 2 * ROUTER_STEPS)
            for e in range(2):
                nc.vector.tensor_copy(gate_now[:, e, QT:NT].unsqueeze(1), gates_e[:, e:e + 1, QT:NT])\
                  .then_inc(gates_late, 1)
            dve.wait_ge(gates_late, 2)
            dve.wait_ge(b2_read, NB * B)
            for k in range(4, 8):
                add_up(dve, k, *FIRST_TILES[k])

            def expert(e, par):
                for n in range(NB * B):
                    add_up(dve, e * 4 + n, par, n)

            def take_gates(e, par, at):
                nc.vector.tensor_copy(b1_now[:, par, :].unsqueeze(1), be[:, at, :])
                nc.vector.tensor_copy(gate_now[:, par, :].unsqueeze(1), gates_e[:, at, :]).then_inc(gate_copied, 1)
                dve.wait_ge(gate_copied, e + 1)

            with dve.Fori(1, E // 2) as i:
                for par in range(2):
                    e = i * 2 + par
                    take_gates(e, par, bass.ds(e, 1))
                    expert(e, par)
            take_gates(E, 0, slice(E, E + 1))
            expert(E, 0)
            dve.wait_ge(acc_done, EXPERTS * 4 + 2)
            nc.vector.scalar_tensor_tensor(acc[:, :, :], acc[:, :, :], MOE_SCALE, h[:, :, :], ALU.mult, ALU.add)\
              .then_inc(finished, 1)


def bf16_bits(a):
    b = np.ascontiguousarray(a, np.float32).view(np.uint32)
    return ((b + np.uint32(0x7fff) + ((b >> 16) & np.uint32(1))) >> 16).astype(np.uint16)


def rounded(a):
    return (bf16_bits(a).astype(np.uint32) << 16).view(np.float32)


def constants():
    half = DH // 2
    inv = (1.0 / np.float32(10000.0) ** (np.arange(0, DH, 2, dtype=np.float32) / DH)).astype(np.float32)
    angle = np.arange(S, dtype=np.float64)[None, :] * inv.astype(np.float64)[:, None]
    sin, cos = np.sin(angle), np.cos(angle)
    ch = ORDER % DH
    f = ch % half
    rot = np.stack([sin[f], np.where((ch < half)[:, None], cos[f], -cos[f])], axis=1).astype(np.float32)
    table = np.concatenate([cos, sin], axis=0).astype(np.float32)
    high = rounded(table)
    middle = rounded(table - high)
    low = rounded(table - high - middle)
    parts = (high, middle, low)
    kst = np.concatenate([parts[i] for i in K_PARTS] + [np.ones((2, S), np.float32)], axis=0)
    ident = np.eye(P, dtype=np.float32)
    mask = np.where(np.arange(P)[None, :] > np.arange(P)[:, None], np.float32(NEG), np.float32(0))
    return ident, bf16_bits(ident), bf16_bits(mask), rot, bf16_bits(kst)


def kernel(**inp):
    import concourse.bacc as bacc
    from concourse.bass_utils import run_bass_kernel_spmd
    a = {k: np.asarray(v) for k, v in inp.items()}
    A = {k[8:]: v for k, v in a.items() if k.startswith("L0_attn_")}
    M = {k[7:]: v for k, v in a.items() if k.startswith("L0_ffn_")}
    swap = ORDER.reshape(NQ, 2, DH // 2, G)[:, ::-1].reshape(P)
    t = lambda w: np.swapaxes(w, -1, -2)
    u = A["u_bias"].reshape(L, D)
    wa = np.concatenate([t(A["Wq"][:, ORDER]), t(A["Wq"][:, swap]), t(A["Wk"][:, ORDER]), t(A["Wv"])], axis=2)
    va = np.stack([A["bq"][:, ORDER], A["bk"][:, ORDER], u[:, ORDER], A["bq"][:, swap], u[:, swap], A["ln1_w"],
                   A["ln1_b"]], axis=2)
    tiles = lambda w: np.swapaxes(t(w).reshape(w.shape[0], FT, P, D), 1, 2).reshape(w.shape[0], P, FT * D)
    wd = np.concatenate([t(A["Wo"]), t(A["W1"]), tiles(A["W2"])], axis=2)
    vd = np.concatenate([np.stack([A["bv"], A["ln2_w"], A["ln2_b"]], axis=2),
                         np.swapaxes(A["b1"].reshape(L, FT, P), 1, 2), A["bv"][:, :, None]], axis=2)
    rows = np.concatenate([A["bo"], A["b2"]], axis=1)
    w1 = np.concatenate([t(M["W1"]), t(M["Ws1"])[None]], axis=0)
    w2 = np.concatenate([tiles(M["W2"]), tiles(M["Ws2"][None])], axis=0)
    we = np.concatenate([w1, w2], axis=2)
    b1 = np.concatenate([M["b1"], M["bs1"][None]], axis=0).reshape(EXPERTS, FT, P)
    b2 = np.concatenate([M["b2"], M["bs2"][None]], axis=0)
    be = np.concatenate([b2, np.swapaxes(b1, 1, 2).reshape(EXPERTS, FF)], axis=1)
    given = {"x": A["x"], "wa": wa, "va": va, "wd": wd, "vd": vd, "rows": rows, "wr": t(M["w_router"]), "we": we,
             "be": be}
    given |= dict(zip(("ident", "ident_b", "mask_b", "rot", "kst"), constants()))
    nc = bacc.Bacc("TRN2", target_bir_lowering=False, num_devices=1)
    arrays, args = {}, []
    for name, v in given.items():
        v = np.ascontiguousarray(v)
        arrays[f"in_{name}"] = v
        ap = nc.dram_tensor(f"in_{name}", v.shape, mybir.dt.from_np(v.dtype), kind="ExternalInput").ap()
        args.append(ap.bitcast(BF16) if v.dtype == np.uint16 else ap)
    args.append(nc.dram_tensor("out", (B, S, D), F32, kind="ExternalOutput").ap())
    build(nc, *args)
    r = run_bass_kernel_spmd(nc, [arrays], core_ids=[0])
    return r.results[0]["out"]
```
